# Optimizing a Trainium2 kernel written in Bass

```python
import numpy as np
import jax
import jax.numpy as jnp

def _softmax(x, axis=-1):
    return jax.nn.softmax(x, axis=axis)

def _gelu(x):
    return jax.nn.gelu(x, approximate=True)

def _silu(x):
    return jax.nn.silu(x)

def _sigmoid(x):
    return jax.nn.sigmoid(x)

def _layernorm(x, axis=-1, eps=1e-05):
    m = jnp.mean(x, axis=axis, keepdims=True)
    v = jnp.var(x, axis=axis, keepdims=True)
    return (x - m) / jnp.sqrt(v + eps)

def _scatter_add(tgt, idx, src, axis=0):
    return tgt.at[idx].add(src)

def _segment_sum(src, seg, n):
    return jax.ops.segment_sum(src, seg, n)
kernel_name = 'mk_gps_d1_gnn_r8_a39a78'

def setup_inputs(seed: int=0):
    np.random.seed(seed)
    _w = jnp.asarray

    def _rec_inputs():
        import jax
        import jax.numpy as jnp
        _gk = jax.random.key(seed)
        x = -0.0003713 + 1 * jax.random.normal(jax.random.fold_in(_gk, 1), (6250, 256), jnp.float32)
        src = jax.random.randint(jax.random.fold_in(_gk, 2), (100000,), 0, 6250, jnp.int32)
        dst = jnp.minimum((6250 * jax.random.uniform(jax.random.fold_in(_gk, 3), (100000,)) ** 2.0).astype(jnp.int32), 49999)
        _o = jnp.argsort(dst, stable=True)
        src = src[_o]
        dst = dst[_o]
        return (x, src, dst)
    x, src, dst = _rec_inputs()

    def _L0_gnn_setup():
        import jax, jax.numpy as jnp
        import numpy as np
        N, E, IN, OUT = (6250, 100000, 256, 256)
        EPS = 1e-05
        key = jax.random.key(seed)
        k1, k2, k3 = jax.random.split(key, 3)
        x = jax.random.normal(k1, (N, IN), dtype=jnp.float32)
        edge_index = jax.random.randint(k2, (2, E), 0, N, dtype=jnp.int64)
        batch = jnp.zeros((N,), dtype=jnp.int64)
        scale = jnp.sqrt(2.0 / (IN + OUT)).astype(jnp.float32)
        W = jax.random.normal(k3, (IN, OUT), dtype=jnp.float32) * scale
        conv_bias = jnp.zeros((OUT,), dtype=jnp.float32)
        ln_weight = jnp.ones((OUT,), dtype=jnp.float32)
        ln_bias = jnp.zeros((OUT,), dtype=jnp.float32)
        prelu_a = jnp.full((1,), 0.25, dtype=jnp.float32)
        return {'x': x, 'edge_index': edge_index, 'batch': batch, 'W': W, 'conv_bias': conv_bias, 'ln_weight': ln_weight, 'ln_bias': ln_bias, 'prelu_a': prelu_a}
    _L0_gnn_all = _L0_gnn_setup()
    _L0_gnn_in = {k: v for k, v in _L0_gnn_all.items() if k in ('W', 'conv_bias', 'ln_weight', 'ln_bias', 'prelu_a')}
    del _L0_gnn_all

    def _L0_mix_setup():
        import jax, jax.numpy as jnp
        import numpy as np
        DIM = 256
        HEADS = 4
        DIM_HEAD = 32
        NUM_MEM = 4
        HIDDEN = HEADS * DIM_HEAD
        SCALE = DIM_HEAD ** (-0.5)

        def rmsnorm(x, g):
            n = jnp.linalg.norm(x, axis=-1, keepdims=True)
            return x / jnp.maximum(n, 1e-12) * g * x.shape[-1] ** 0.5
        key = jax.random.key(seed)
        ks = jax.random.split(key, 8)
        B, N = (4, 2048)
        return {'x': jax.random.normal(ks[0], (B, N, DIM), jnp.float32), 't': jax.random.normal(ks[1], (B,), jnp.float32), 'w_qkv': jax.random.normal(ks[2], (DIM, 3 * HIDDEN), jnp.float32) * 0.02, 'mem_kv': jax.random.normal(ks[3], (2, HEADS, DIM_HEAD, NUM_MEM), jnp.float32), 'w_out': jax.random.normal(ks[4], (HIDDEN, DIM), jnp.float32) * 0.02, 'b_out': jnp.zeros((DIM,), jnp.float32), 'g_out': jnp.ones((DIM,), jnp.float32), 'g_pre': jnp.ones((DIM,), jnp.float32)}
    _L0_mix_all = _L0_mix_setup()
    _L0_mix_in = {k: v for k, v in _L0_mix_all.items() if k in ('t', 'w_qkv', 'mem_kv', 'w_out', 'b_out', 'g_out', 'g_pre')}
    del _L0_mix_all

    def _L0_ffn_setup():
        import jax, jax.numpy as jnp
        import numpy as np
        E = 8
        K = 2
        D = 256
        H = 512
        DOUT = 256
        EPS = 1e-05
        key = jax.random.key(seed)
        ks = jax.random.split(key, 9)
        s = 0.02
        return {'x': jax.random.normal(ks[0], (4, 1024, D), jnp.float32), 'gamma': 1.0 + 0.05 * jax.random.normal(ks[1], (D,), jnp.float32), 'beta': 0.05 * jax.random.normal(ks[2], (D,), jnp.float32), 'Wr': 0.01 * jax.random.normal(ks[3], (D, E), jnp.float32), 'br': jnp.zeros((E,), jnp.float32), 'W1': s * jax.random.normal(ks[4], (E, D, H), jnp.float32), 'b1': s * jax.random.normal(ks[5], (E, H), jnp.float32), 'W2': s * jax.random.normal(ks[6], (E, H, DOUT), jnp.float32), 'b2': s * jax.random.normal(ks[7], (E, DOUT), jnp.float32)}
    _L0_ffn_all = _L0_ffn_setup()
    _L0_ffn_in = {k: v for k, v in _L0_ffn_all.items() if k in ('gamma', 'beta', 'Wr', 'br', 'W1', 'b1', 'W2', 'b2')}
    del _L0_ffn_all
    return {'x': x, 'src': src, 'dst': dst, 'L0_gnn_W': _L0_gnn_in['W'], 'L0_gnn_conv_bias': _L0_gnn_in['conv_bias'], 'L0_gnn_ln_weight': _L0_gnn_in['ln_weight'], 'L0_gnn_ln_bias': _L0_gnn_in['ln_bias'], 'L0_gnn_prelu_a': _L0_gnn_in['prelu_a'], 'L0_mix_t': _L0_mix_in['t'], 'L0_mix_w_qkv': _L0_mix_in['w_qkv'], 'L0_mix_mem_kv': _L0_mix_in['mem_kv'], 'L0_mix_w_out': _L0_mix_in['w_out'], 'L0_mix_b_out': _L0_mix_in['b_out'], 'L0_mix_g_out': _L0_mix_in['g_out'], 'L0_mix_g_pre': _L0_mix_in['g_pre'], 'L0_ffn_gamma': _L0_ffn_in['gamma'], 'L0_ffn_beta': _L0_ffn_in['beta'], 'L0_ffn_Wr': _L0_ffn_in['Wr'], 'L0_ffn_br': _L0_ffn_in['br'], 'L0_ffn_W1': _L0_ffn_in['W1'], 'L0_ffn_b1': _L0_ffn_in['b1'], 'L0_ffn_W2': _L0_ffn_in['W2'], 'L0_ffn_b2': _L0_ffn_in['b2']}

def reference(x, src, dst, L0_gnn_W, L0_gnn_conv_bias, L0_gnn_ln_weight, L0_gnn_ln_bias, L0_gnn_prelu_a, L0_mix_t, L0_mix_w_qkv, L0_mix_mem_kv, L0_mix_w_out, L0_mix_b_out, L0_mix_g_out, L0_mix_g_pre, L0_ffn_gamma, L0_ffn_beta, L0_ffn_Wr, L0_ffn_br, L0_ffn_W1, L0_ffn_b1, L0_ffn_W2, L0_ffn_b2):
    import jax
    import jax.numpy as jnp

    def _L0_gnn_ref(x, edge_index, batch, W, conv_bias, ln_weight, ln_bias, prelu_a):
        import jax, jax.numpy as jnp
        import numpy as np
        N, E, IN, OUT = (6250, 100000, 256, 256)
        EPS = 1e-05
        n = x.shape[0]
        src, dst = (edge_index[0], edge_index[1])
        loop = jnp.arange(n, dtype=src.dtype)
        src_f = jnp.concatenate([src, loop])
        dst_f = jnp.concatenate([dst, loop])
        h = x @ W
        deg = jax.ops.segment_sum(jnp.ones_like(dst_f, dtype=h.dtype), dst_f, num_segments=n)
        dinv = jax.lax.rsqrt(deg)
        norm = dinv[src_f] * dinv[dst_f]
        out = jax.ops.segment_sum(h[src_f] * norm[:, None], dst_f, num_segments=n) + conv_bias
        mu = out.mean()
        xc = out - mu
        std = jnp.sqrt((xc * xc).mean())
        y = xc / (std + EPS) * ln_weight + ln_bias
        return jnp.where(y >= 0, y, prelu_a * y)

    def _L0_mix_ref(x, t, w_qkv, mem_kv, w_out, b_out, g_out, g_pre):
        import jax, jax.numpy as jnp
        import numpy as np
        DIM = 256
        HEADS = 4
        DIM_HEAD = 32
        NUM_MEM = 4
        HIDDEN = HEADS * DIM_HEAD
        SCALE = DIM_HEAD ** (-0.5)

        def rmsnorm(x, g):
            n = jnp.linalg.norm(x, axis=-1, keepdims=True)
            return x / jnp.maximum(n, 1e-12) * g * x.shape[-1] ** 0.5
        b, n, c = x.shape
        xn = rmsnorm(x, g_pre)
        qkv = xn @ w_qkv
        q, k, v = jnp.split(qkv, 3, axis=-1)

        def to_heads(z):
            return z.reshape(b, n, HEADS, DIM_HEAD).transpose(0, 2, 3, 1)
        q, k, v = map(to_heads, (q, k, v))
        mk = jnp.broadcast_to(mem_kv[0], (b, HEADS, DIM_HEAD, NUM_MEM))
        mv = jnp.broadcast_to(mem_kv[1], (b, HEADS, DIM_HEAD, NUM_MEM))
        k = jnp.concatenate([mk, k], axis=-1)
        v = jnp.concatenate([mv, v], axis=-1)
        q = jax.nn.softmax(q, axis=-2) * SCALE
        k = jax.nn.softmax(k, axis=-1)
        context = jnp.einsum('bhdn,bhen->bhde', k, v)
        out = jnp.einsum('bhde,bhdn->bhen', context, q)
        out = out.transpose(0, 3, 1, 2).reshape(b, n, HIDDEN)
        out = rmsnorm(out @ w_out + b_out, g_out)
        return out + x

    def _L0_ffn_ref(x, gamma, beta, Wr, br, W1, b1, W2, b2):
        import jax, jax.numpy as jnp
        import numpy as np
        E = 8
        K = 2
        D = 256
        H = 512
        DOUT = 256
        EPS = 1e-05
        mu = jnp.mean(x, axis=-1, keepdims=True)
        var = jnp.mean(jnp.square(x - mu), axis=-1, keepdims=True)
        xn = (x - mu) * jax.lax.rsqrt(var + EPS) * gamma + beta
        logits = jnp.einsum('bsd,de->bse', xn, Wr) + br
        top_vals, top_idx = jax.lax.top_k(logits, K)
        w = jax.nn.softmax(top_vals, axis=-1)
        w_full = jnp.einsum('bsk,bske->bse', w, jax.nn.one_hot(top_idx, E, dtype=w.dtype))
        y = jnp.zeros(x.shape[:-1] + (DOUT,), x.dtype)
        for e in range(E):
            h = jax.nn.gelu(jnp.einsum('bsd,dh->bsh', xn, W1[e]) + b1[e], approximate=False)
            y_e = jnp.einsum('bsh,hd->bsd', h, W2[e]) + b2[e]
            y = y + y_e * w_full[..., e, None]
        return y
    edge_index = jnp.stack([src, dst])
    batch0 = jnp.zeros((6250,), jnp.int32)
    xn = _layernorm(x, axis=-1)
    x = x + _L0_gnn_ref(xn, edge_index, batch0, L0_gnn_W, L0_gnn_conv_bias, L0_gnn_ln_weight, L0_gnn_ln_bias, L0_gnn_prelu_a) + _L0_mix_ref(xn[None], L0_mix_t, L0_mix_w_qkv, L0_mix_mem_kv, L0_mix_w_out, L0_mix_b_out, L0_mix_g_out, L0_mix_g_pre)[0]
    x = x + _L0_ffn_ref(_layernorm(x, axis=-1)[None], L0_ffn_gamma, L0_ffn_beta, L0_ffn_Wr, L0_ffn_br, L0_ffn_W1, L0_ffn_b1, L0_ffn_W2, L0_ffn_b2)[0]
    return x

_drawn_inputs = setup_inputs


def setup_inputs(seed=0):
    import zlib

    import numpy as np

    out = dict(_drawn_inputs(seed))
    spreads = {'L0_gnn_conv_bias': (0.0, 0.1),
     'L0_gnn_ln_weight': (1.0, 0.2),
     'L0_gnn_ln_bias': (0.0, 0.1),
     'L0_mix_b_out': (0.0, 0.1),
     'L0_mix_g_out': (1.0, 0.2),
     'L0_mix_g_pre': (1.0, 0.6),
     'L0_ffn_br': (0.0, 0.384)}
    factors = {'L0_mix_w_qkv': 8.0,
     'L0_mix_mem_kv': 8.0,
     'L0_mix_w_out': 8.0,
     'L0_ffn_gamma': 8.0,
     'L0_ffn_beta': 8.0,
     'L0_ffn_Wr': 3.719,
     'L0_ffn_b1': 23.891,
     'L0_ffn_b2': 8.0}
    for name, (base, spread) in spreads.items():
        noise = np.random.default_rng([zlib.crc32(name.encode()), seed]).standard_normal(out[name].shape)
        drawn = base * np.exp(spread * noise) if base else spread * noise
        out[name] = jnp.asarray(drawn.astype(out[name].dtype))
    for name, factor in factors.items():
        out[name] = (out[name] * factor).astype(out[name].dtype)
    return out
```

```python
import concourse.bass as bass
from concourse import mybir
from contextlib import ExitStack

f32, i32, bf16 = mybir.dt.float32, mybir.dt.int32, mybir.dt.bfloat16
ALU, ACT, AX = mybir.AluOpType, mybir.ActivationFunctionType, mybir.AxisListType
P = 128

N, E, D = 6250, 100000, 256
NX, HID, EPS = 8, 512, 1e-5
HEADS, DH, MEM = 4, 32, 4
KC = D // P
HC = HID // P
T = -(-N // P)
TAIL = N - (T - 1) * P
NP = T * P
GC = 4
GE = GC * P
NG = -(-E // GE)
GH = NG // 2
WIN = 96
NC = NG * GC
OHC = 14
OHB = NC // OHC
ACCW = (N // WIN + 1) * WIN + 16
assert ACCW >= N + WIN and NG == 2 * GH and NG == 4 * T and NC % (2 * OHC) == 0 and T % 4 == 1
PADNODE = 8191
SW = -(-N // WIN)
NTILE = (2 * N + NX * (P - 1)) // P
NSTEP = NTILE + 1
assert (NTILE - 1) % 4 == 0
IB = 7
assert 2 * T == 14 * IB
UN = 4
U = T // UN
KVW = 257
W1ROW = KC * HID + HC


def build(nc, a_x, a_src, a_dst, a_gw, a_cb, a_lnw, a_lnb, a_pre, a_wqkv, a_mk, a_mv, a_wout, a_bout,
          a_gout, a_gpre, a_gamma, a_beta, a_wr, a_br, a_w1, a_w2, a_b2, a_out):
    table = nc.dram_tensor("table", (N, D), f32, kind="Internal").ap()
    results = nc.dram_tensor("results", (2 * N + NTILE * P, D), f32, kind="Internal").ap()
    with ExitStack() as ctx:
        def sb(name, shape, dt=f32):
            return ctx.enter_context(nc.sbuf_tensor(name, shape, dt))

        def semaphore(phase, name):
            phase.append(nc.alloc_semaphore(name))
            return phase[-1]

        def over(phase):
            nc.clear_and_free_semaphores(phase)
            nc.all_engine_barrier()

        R1 = sb("R1", [P, T * KVW])
        R2 = sb("R2", [P, KC * NP])
        R3 = sb("R3", [P, KC * ACCW])
        RG = sb("RG", [P, 4 * W1ROW])
        x_all = R1[:, 0:T * D].rearrange("p (t f) -> p t f", f=D)
        kv = R1[:, :].rearrange("p (t f) -> p t f", f=KVW)
        o_all = x_all
        zT = R2[:, :].rearrange("p (k n) -> p k n", k=KC)
        y_all = R2[:, :].rearrange("p (t f) -> p t f", f=D)
        acc = R3[:, :].rearrange("p (k n) -> p k n", k=KC)
        grows = RG[:, 0:16 * D].rearrange("p (s f) -> p s f", f=D)

        dstrel = sb("dstrel", [P, NG + 1, GC])
        dslow = sb("dslow", [P, NG, GC])
        srci = sb("srci", [P, NG, GC], i32)
        idxb = sb("idxb", [P, 2, 16], i32)
        base_i = sb("base_i", [1, NG], i32)
        flag_i = sb("flag_i", [1, 1], i32)
        ident = sb("ident", [P, P])
        ones = sb("ones", [P, P])
        tri = sb("tri", [P, P])
        bmask = sb("bmask", [P, P])
        iwin = sb("iwin", [P, P])
        valid = sb("valid", [P, 1])
        negbig = sb("negbig", [P, 1])
        wqkv = sb("wqkv", [P, KC, 384])
        gw = sb("gw", [P, KC, D])
        gpre = sb("gpre", [P, KC])
        gamma = sb("gamma", [P, KC])
        beta = sb("beta", [P, KC])
        wr = sb("wr", [P, KC, NX])
        wout = sb("wout", [P, D])
        cw = sb("cw", [P, D])
        bout = sb("bout", [P, D])
        gout = sb("gout", [P, D])
        cbias = sb("cbias", [P, D])
        lnw = sb("lnw", [P, D])
        lnb = sb("lnb", [P, D])
        pre = sb("pre", [P, 1])
        brr = sb("brr", [P, NX])
        mk = sb("mk", [P, MEM])
        mvv = sb("mvv", [P, MEM])
        stats = sb("stats", [P, T, 6])
        mv = sb("mv", [P, T, 2])
        deg = sb("deg", [P, T])
        dinv = sb("dinv", [P, T])
        rstd = sb("rstd", [P, T])
        zs_s = sb("zs_s", [P, T])
        zs_b = sb("zs_b", [P, T])
        cq = sb("cq", [P, T])
        x1s = sb("x1s", [P, T])
        x1b = sb("x1b", [P, T])
        ssq = sb("ssq", [P, T])
        sa = sb("sa", [P, T])
        sc = sb("sc", [P, T])
        sd = sb("sd", [P, T])
        slot = sb("slot", [P, 4, D])
        slotb = sb("slotb", [P, 2, D])
        ksl = sb("ksl", [P, 2, P])
        esl = sb("esl", [P, 2, 132])
        qsl = sb("qsl", [P, 2, P])
        qtl = sb("qtl", [P, 2, P])
        small = sb("small", [P, 64])
        S_t = sb("S_t", [P, 2, GC, WIN])

        ps = [ctx.enter_context(nc.psum_tensor(f"ps{i}", [P, 512], f32)) for i in range(8)]

        def window(k):
            return ps[k][:, 0:KC * WIN].rearrange("p (h w) -> p h w", h=KC)

        class Chain:

            def __init__(self, eng, s, start=0):
                self.eng, self.s, self.n = eng, s, start

            def done(self, ins):
                self.n = self.n + 1
                ins.then_inc(self.s, 1)
                self.eng.wait_ge(self.s, self.n)

        dst_ld = R3[:, 0:1024].bitcast(i32).rearrange("p (h e) -> p h e", h=2)
        src_ld = R3[:, 1024:2048].bitcast(i32).rearrange("p (h e) -> p h e", h=2)
        dstf = R3[:, 2048:3072].rearrange("p (h e) -> p h e", h=2)
        relf = R3[:, 3072:4096].rearrange("p (h e) -> p h e", h=2)
        srcf = R3[:, 4096:5120].rearrange("p (h e) -> p h e", h=2)
        tmpf = R3[:, 5120:6144].rearrange("p (h e) -> p h e", h=2)
        dT = R3[:, 6144:6144 + NC].rearrange("p (g c) -> p g c", c=GC)
        dTi = R3[:, 7000:7000 + NC].bitcast(i32)
        hiI = R3[:, 7800:7800 + NC].bitcast(i32)
        loI = R3[:, 8600:8600 + NC].bitcast(i32)
        hiB = R3[:, 9400:9400 + NC // 2].bitcast(bf16)
        loB = R3[:, 9800:9800 + NC // 2].bitcast(bf16)
        iox = RG[:, 0:P * OHC // 2].bitcast(bf16).rearrange("p (j c) -> p j c", c=OHC)
        ohlo = [RG[:, 1000 + 1300 * k:1000 + 1300 * k + P * OHC // 2].bitcast(bf16)
                .rearrange("p (j c) -> p j c", c=OHC) for k in range(2)]
        ohhi = [RG[:, 1900 + 1300 * k:1900 + 1300 * k + T * OHC // 2].bitcast(bf16)
                .rearrange("p (j c) -> p j c", c=OHC) for k in range(2)]
        zeroB = slotb[:, 0, 0:P // 2].bitcast(bf16)
        iwin_i = slotb[:, 1, 0:P].bitcast(i32)
        cols = sb("cols", [P, 8])
        FULL = GH * GE
        LASTG = E - (NG - 1) * GE

        phase = []
        with nc.Block() as block:
            pads = semaphore(phase, "p_pads")
            e_in = semaphore(phase, "p_edges_in")
            x_in = [semaphore(phase, f"p_x_in{k}") for k in range(7)]
            w_in = semaphore(phase, "p_weights_in")
            const = semaphore(phase, "p_const")
            dv = semaphore(phase, "p_dve_order")
            pl = semaphore(phase, "p_pool_order")
            rel_ok = semaphore(phase, "p_rel_ready")
            tr_ok = semaphore(phase, "p_transposed")
            tr_ev = semaphore(phase, "p_transposed_copied")
            bt_ok = semaphore(phase, "p_base_transposed")
            oh_ok = semaphore(phase, "p_onehots_ready")
            oh_free = semaphore(phase, "p_onehots_free")
            deg_ok = semaphore(phase, "p_deg_ready")
            root_in = semaphore(phase, "p_root_in")
            root_ok = semaphore(phase, "p_root_done")
            aff_ok = semaphore(phase, "p_affine_ready")
            z_ok = semaphore(phase, "p_z_ready")
            z_free = semaphore(phase, "p_z_free")
            zt_ps = semaphore(phase, "p_zT_psum")
            zt_ok = semaphore(phase, "p_zT_copied")
            tw = [semaphore(phase, f"p_table{k}") for k in range(4)]

            @block.sync
            def _(sp):
                sp.wait_ge(pads, 2)
                for src_, dst_ in ((a_dst, dst_ld), (a_src, src_ld)):
                    sp.dma_start(dst_[0:GH, 0, :], src_[0:FULL].rearrange("(p e) -> p e", e=GE)).then_inc(e_in, 16)
                    sp.dma_start(dst_[0:GH - 1, 1, :],
                                 src_[FULL:2 * FULL - GE].rearrange("(p e) -> p e", e=GE)).then_inc(e_in, 16)
                    sp.dma_start(dst_[GH - 1:GH, 1, 0:LASTG],
                                 src_[2 * FULL - GE:E].rearrange("(p e) -> p e", p=1)).then_inc(e_in, 16)
                sp.wait_ge(pads, 3)
                for k in range(7):
                    lo, hi = 7 * k, min(7 * k + 7, T - 1)
                    sp.dma_start(x_all[:, lo:hi, :],
                                 a_x[lo * P:hi * P, :].rearrange("(t p) f -> p t f", p=P)).then_inc(x_in[k], 16)
                sp.dma_start(x_all[0:TAIL, T - 1, :], a_x[(T - 1) * P:N, :]).then_inc(x_in[6], 16)
                with nc.sync.Fori(0, U) as i:
                    for u in range(UN):
                        sp.wait_ge(z_ok, i * UN + (u + 1))
                        sp.dma_start(table[bass.ds((i * UN + u) * P, P), :], slot[:, u, :]).then_inc(tw[u], 16)
                sp.wait_ge(z_ok, T)
                sp.dma_start(table[(T - 1) * P:N, :], slot[0:TAIL, 0, :]).then_inc(tw[0], 16)
                for u in range(UN):
                    sp.wait_ge(tw[u], 16 * (U + (1 if u == 0 else 0)))

            @block.scalar
            def _(act):
                for d_, s_ in (
                    (wqkv[:, :, :], a_wqkv.rearrange("(k p) n -> p k n", p=P)),
                    (gw[:, :, :], a_gw.rearrange("(k p) n -> p k n", p=P)),
                    (gpre[:, :], a_gpre.rearrange("(p k) -> p k", k=KC)),
                    (gamma[:, :], a_gamma.rearrange("(p k) -> p k", k=KC)),
                    (beta[:, :], a_beta.rearrange("(p k) -> p k", k=KC)),
                    (wr[:, :, :], a_wr.rearrange("(k p) n -> p k n", p=P)),
                    (wout[:, :], a_wout),
                    (bout[:, :], a_bout.unsqueeze(0).to_broadcast([P, D])),
                    (gout[:, :], a_gout.unsqueeze(0).to_broadcast([P, D])),
                    (cbias[:, :], a_cb.unsqueeze(0).to_broadcast([P, D])),
                    (lnw[:, :], a_lnw.unsqueeze(0).to_broadcast([P, D])),
                    (lnb[:, :], a_lnb.unsqueeze(0).to_broadcast([P, D])),
                    (pre[:, :], a_pre.unsqueeze(0).to_broadcast([P, 1])),
                    (brr[:, :], a_br.unsqueeze(0).to_broadcast([P, NX])),
                    (mk[:, :], a_mk), (mvv[:, :], a_mv),
                ):
                    act.dma_start(d_, s_).then_inc(w_in, 16)
                for n, dest in enumerate((dT, dstrel, srci)):
                    for h in range(2):
                        act.wait_ge(tr_ok, 2 * n + h + 1)
                        act.activation(dest[:, h * GH:(h + 1) * GH, :].rearrange("p g c -> p c g"),
                                       ps[2 * n + h][:, 0:GC * GH].rearrange("p (c g) -> p c g", c=GC),
                                       ACT.Copy).then_inc(tr_ev, 1)
                act.wait_ge(root_in, 1)
                act.activation(sa[:, :], sc[:, :], ACT.Sqrt).then_inc(root_ok, 1)
                act.wait_ge(root_in, 2)
                act.activation(sa[:, :], sc[:, :], ACT.Sqrt).then_inc(root_ok, 1)
                act.wait_ge(root_in, 3)
                act.activation(sa[:, :], sc[:, :], ACT.Sqrt).then_inc(root_ok, 1)
                act.wait_ge(aff_ok, 1)
                act.sem_inc(z_free, UN)

                def z_tile(t, u):
                    act.wait_ge(z_free, t + 1)
                    act.activation(slot[:, u, :], x_all[:, bass.ds(t, 1), :].rearrange("p a f -> p (a f)"),
                                   ACT.Identity, bias=zs_b[:, bass.ds(t, 1)],
                                   scale=zs_s[:, bass.ds(t, 1)]).then_inc(z_ok, 1)

                with nc.scalar.Fori(0, U) as i:
                    for u in range(UN):
                        z_tile(i * UN + u, u)
                z_tile(T - 1, 0)

            @block.gpsimd
            def _(pool):
                n = 0

                def step(ins):
                    nonlocal n
                    n += 1
                    ins.then_inc(pl, 1)
                    pool.wait_ge(pl, n)

                step(nc.gpsimd.memset(ident[:, :], 0.0))
                step(nc.gpsimd.affine_select(out=ident[:, :], in_=ident[:, :], compare_op=ALU.not_equal, fill=1.0,
                                             base=0, pattern=[[-1, P]], channel_multiplier=1))
                pool.sem_inc(const, 1)
                step(nc.gpsimd.iota(iox[:, :, :], pattern=[[1, P], [0, OHC]], base=0, channel_multiplier=0,
                                    allow_small_or_imprecise_dtypes=True))
                step(nc.gpsimd.iota(iwin_i, pattern=[[1, P]], base=0, channel_multiplier=0))
                step(nc.gpsimd.tensor_copy(iwin[:, :], iwin_i))
                pool.sem_inc(const, 1)
                step(nc.gpsimd.memset(ones[:, :], 1.0))
                step(nc.gpsimd.affine_select(out=tri[:, :], in_=ones[:, :], compare_op=ALU.is_gt, fill=0.0,
                                             base=0, pattern=[[1, P]], channel_multiplier=-1))
                step(nc.gpsimd.affine_select(out=valid[:, :], in_=ones[:, 0:1], compare_op=ALU.is_gt, fill=0.0,
                                             base=TAIL, pattern=[[0, 1]], channel_multiplier=-1))
                step(nc.gpsimd.memset(bmask[:, :], 0.0))
                for h in range(HEADS):
                    step(nc.gpsimd.memset(bmask[h * DH:(h + 1) * DH, h * DH:(h + 1) * DH], 1.0))
                pool.sem_inc(const, 1)
                pool.wait_ge(deg_ok, 1)
                pool.wait_ge(zt_ok, T + 2)
                nc.gpsimd.memset(acc[:, :, N:ACCW], 0.0).then_inc(pl, 1)
                nc.gpsimd.tensor_copy(acc[:, :, 0:N], zT[:, :, 0:N]).then_inc(pl, 1)
                pool.wait_ge(pl, n + 2)

            @block.tensor
            def _(pe):
                pe.sem_inc(oh_free, 2)
                pe.sem_inc(zt_ok, 2)
                pe.wait_ge(const, 1)
                for n, arr in enumerate((dstf, relf, srcf)):
                    pe.wait_ge(rel_ok, n + 1)
                    for h in range(2):
                        for c in range(GC):
                            last = nc.tensor.transpose(ps[2 * n + h][:, c * GH:(c + 1) * GH],
                                                       arr[0:GH, h, c * P:(c + 1) * P], ident[0:GH, 0:GH])
                        last.then_inc(tr_ok, 1)
                pe.wait_ge(rel_ok, 4)
                for k in range(4):
                    last = nc.tensor.transpose(ps[6][0:1, k * GH:(k + 1) * GH], cols[0:GH, k:k + 1],
                                               ident[0:GH, 0:GH])
                last.then_inc(bt_ok, 1)
                pe.wait_ge(oh_ok, 1)
                nc.tensor.matmul(ps[7][:, 0:T], zeroB, zeroB[:, 0:T], start=True, stop=False)
                with nc.tensor.Fori(0, OHB // 2) as i:
                    for k in range(2):
                        pe.wait_ge(oh_ok, i * 2 + (k + 2))
                        for c in range(OHC):
                            last = nc.tensor.matmul(ps[7][:, 0:T], ohlo[k][:, :, c], ohhi[k][:, :, c],
                                                    start=False, stop=False)
                        last.then_inc(oh_free, 1)
                nc.tensor.matmul(ps[7][:, 0:T], zeroB, zeroB[:, 0:T], start=False, stop=True).then_inc(deg_ok, 1)

                def flip(t, u):
                    pe.wait_ge(z_ok, t + 1)
                    pe.wait_ge(zt_ok, t + 1)
                    for k in range(KC):
                        last = nc.tensor.transpose(ps[u % 2][:, k * P:(k + 1) * P], slot[:, u, k * P:(k + 1) * P],
                                                   ident[:, :])
                    last.then_inc(zt_ps, 1)

                with nc.tensor.Fori(0, U) as i:
                    for u in range(UN):
                        flip(i * UN + u, u)
                flip(T - 1, 0)

            @block.vector
            def _(v):
                nc.vector.memset(dst_ld[:, 1, :], PADNODE).then_inc(pads, 1)
                nc.vector.memset(src_ld[:, 1, :], 0).then_inc(pads, 1)
                nc.vector.memset(x_all[:, T - 1, :], 0.0).then_inc(pads, 1)
                nc.vector.memset(dstrel[:, NG, :], -1.0)
                nc.vector.memset(zeroB, 0.0).then_inc(oh_ok, 1)
                ch = Chain(v, dv)
                v.wait_ge(e_in, 16 * 6)
                h = slice(0, GH)
                ch.done(nc.vector.tensor_copy(dstf[h, :, :], dst_ld[h, :, :]))
                v.sem_inc(rel_ok, 1)
                ch.done(nc.vector.tensor_reduce(cols[h, 0:2], dstf[h, :, :], AX.X, ALU.min))
                for k in range(2):
                    ch.done(nc.vector.tensor_scalar(relf[h, k, :], dstf[h, k, :], cols[h, k:k + 1], None,
                                                    ALU.subtract))
                v.sem_inc(rel_ok, 1)
                ch.done(nc.vector.tensor_copy(srcf[h, :, :], src_ld[h, :, :]))
                v.sem_inc(rel_ok, 1)
                ch.done(nc.vector.tensor_scalar(tmpf[h, :, :], dstf[h, :, :], float(N), None, ALU.is_lt))
                ch.done(nc.vector.tensor_tensor(tmpf[h, :, :], tmpf[h, :, :], relf[h, :, :], ALU.mult))
                ch.done(nc.vector.tensor_reduce(cols[h, 2:4], tmpf[h, :, :], AX.X, ALU.max))
                v.sem_inc(rel_ok, 1)
                v.wait_ge(tr_ev, 2)
                dflat = dT.rearrange("p g c -> p (g c)")
                ch.done(nc.vector.tensor_copy(dTi, dflat))
                ch.done(nc.vector.tensor_scalar(hiI, dTi, 7, None, ALU.arith_shift_right))
                ch.done(nc.vector.tensor_scalar(loI, dTi, P - 1, None, ALU.bitwise_and))
                ch.done(nc.vector.tensor_copy(hiB, hiI))
                ch.done(nc.vector.tensor_copy(loB, loI))
                v.wait_ge(tr_ev, 4)
                ch.done(nc.vector.tensor_scalar(dslow[:, :, :], dstrel[:, 0:NG, :], float(WIN), -1e6, ALU.is_lt,
                                                ALU.mult))
                ch.done(nc.vector.tensor_tensor(dslow[:, :, :], dslow[:, :, :], dT, ALU.add))
                v.wait_ge(bt_ok, 1)
                ch.done(nc.vector.tensor_copy(base_i[0:1, :], ps[6][0:1, 0:NG]))
                ch.done(nc.vector.tensor_reduce(small[0:1, 0:1], ps[6][0:1, NG:2 * NG], AX.X, ALU.max))
                ch.done(nc.vector.tensor_scalar(flag_i[0:1, :], small[0:1, 0:1], float(WIN), None, ALU.is_ge))
                v.wait_ge(const, 2)

                order = ch.n
                with nc.vector.Fori(0, OHB // 2) as i:
                    for k in range(2):
                        m = i * 2 + k
                        v.wait_ge(oh_free, m + 1)
                        lo = loB[:, bass.ds(m * OHC, OHC)].unsqueeze(1)
                        hi = hiB[:, bass.ds(m * OHC, OHC)].unsqueeze(1)
                        nc.vector.tensor_tensor(ohlo[k], lo.to_broadcast([P, P, OHC]), iox, ALU.is_equal)
                        nc.vector.tensor_tensor(ohhi[k], hi.to_broadcast([P, T, OHC]), iox[:, 0:T, :],
                                                ALU.is_equal).then_inc(oh_ok, 1)
                for k in range(7):
                    v.wait_ge(x_in[k], 16 * (2 if k == 6 else 1))
                    for t in range(7 * k, 7 * k + 7):
                        last = nc.vector.bn_stats(stats[:, t, :], x_all[:, t, :])
                last.then_inc(dv, 1)
                ch.n = order + 1
                v.wait_ge(dv, ch.n)
                for t in range(T):
                    last = nc.vector.bn_aggr(mv[:, t, :], stats[:, t, :])
                ch.done(last)

                def rsqrt(out, val, count):
                    v.sem_inc(root_in, 1)
                    v.wait_ge(root_ok, count)
                    ch.done(nc.vector.reciprocal(out, sa[:, :]))
                    ch.done(nc.vector.tensor_tensor(sd[:, :], out, out, ALU.mult))
                    ch.done(nc.vector.tensor_tensor(sd[:, :], sd[:, :], val, ALU.mult))
                    ch.done(nc.vector.tensor_scalar(sd[:, :], sd[:, :], -0.5, 1.5, ALU.mult, ALU.add))
                    ch.done(nc.vector.tensor_tensor(out, out, sd[:, :], ALU.mult))

                mean, var = mv[:, :, 0], mv[:, :, 1]
                ch.done(nc.vector.tensor_scalar(sc[:, :], var, EPS, None, ALU.add))
                rsqrt(rstd[:, :], sc[:, :], 1)
                ch.done(nc.vector.tensor_tensor(sc[:, :], rstd[:, :], rstd[:, :], ALU.mult))
                ch.done(nc.vector.tensor_tensor(sc[:, :], sc[:, :], var, ALU.mult))
                ch.done(nc.vector.tensor_scalar(sc[:, :], sc[:, :], float(D), 1e-24, ALU.mult, ALU.max))
                rsqrt(cq[:, :], sc[:, :], 2)
                v.wait_ge(deg_ok, 1)
                ch.done(nc.vector.tensor_scalar(deg[:, :], ps[7][:, 0:T], 1.0, None, ALU.add))
                ch.done(nc.vector.tensor_copy(sc[:, :], deg[:, :]))
                rsqrt(dinv[:, :], sc[:, :], 3)
                ch.done(nc.vector.tensor_tensor(zs_s[:, :], rstd[:, :], dinv[:, :], ALU.mult))
                ch.done(nc.vector.scalar_tensor_tensor(zs_b[:, :], mean, -1.0, zs_s[:, :], ALU.mult, ALU.mult))
                v.sem_inc(aff_ok, 1)
                ch.done(nc.vector.tensor_tensor(sc[:, :], deg[:, :], dinv[:, :], ALU.mult))
                ch.done(nc.vector.scalar_tensor_tensor(cq[:, :], cq[:, :], float(D) ** 0.5, sc[:, :], ALU.mult,
                                                       ALU.mult))
                ch.done(nc.vector.tensor_scalar(x1s[:, :], rstd[:, :], 1.0, None, ALU.add))
                ch.done(nc.vector.scalar_tensor_tensor(x1b[:, :], mean, -1.0, rstd[:, :], ALU.mult, ALU.mult))
                v.wait_ge(const, 3)
                ch.done(nc.vector.tensor_scalar(negbig[:, :], valid[:, :], 1e30, -1e30, ALU.mult, ALU.add))
                v.wait_ge(w_in, 16 * 16)
                for k in range(KC):
                    ch.done(nc.vector.tensor_scalar(wqkv[:, k, :], wqkv[:, k, :], gpre[:, k:k + 1], None, ALU.mult))

                def keep(t, u):
                    v.wait_ge(zt_ps, t + 1)
                    nc.vector.tensor_copy(zT[:, :, bass.ds(t * P, P)],
                                          ps[u % 2][:, 0:D].rearrange("p (k n) -> p k n", k=KC)).then_inc(zt_ok, 1)
                    v.wait_ge(tw[u], (t - u) * (16 // UN) + 16)
                    v.sem_inc(z_free, 1)

                with nc.vector.Fori(0, U) as i:
                    for u in range(UN):
                        keep(i * UN + u, u)
                v.wait_ge(zt_ps, T)
                nc.vector.tensor_copy(zT[:, :, (T - 1) * P:T * P],
                                      ps[0][:, 0:D].rearrange("p (k n) -> p k n", k=KC)).then_inc(zt_ok, 1)

        over(phase)

        TA, TC = 0, 2 * T
        TB = TC + T
        negM = small[:, 1:2]
        mrow = slotb[:, 0, 0:P]
        emk = small[:, 4:4 + MEM]
        emT = sb("emT", [MEM, P])
        mvT = sb("mvT", [MEM, P + 1])
        cn = slotb[:, 0, P:2 * P]
        cnT = slotb[:, 1, 0:P]
        psA, psC, psT, psO = [ps[2], ps[3]], ps[4], ps[5], [ps[6], ps[7]]

        phase = []
        with nc.Block() as block:
            got = [semaphore(phase, f"a_rows{k}") for k in range(16)]
            idx_ok = semaphore(phase, "a_indices")
            turns = semaphore(phase, "a_turns")
            pe_done = semaphore(phase, "a_group_multiplied")
            s_ok = semaphore(phase, "a_onehots")
            acc_ok = semaphore(phase, "a_group_added")
            zt_ok = semaphore(phase, "a_z_copied")
            mm_ok = semaphore(phase, "a_products")
            kv_ev = semaphore(phase, "a_kv_copied")
            ks_ok = semaphore(phase, "a_keys_less_max")
            ex_ok = semaphore(phase, "a_keys_exp")
            cx_ok = semaphore(phase, "a_context_added")
            m_ps = semaphore(phase, "a_max_transposed")
            m_ok = semaphore(phase, "a_max_ready")
            mem_ok = semaphore(phase, "a_memory_exp")
            mid_pe = semaphore(phase, "a_setup_products")
            mid_dve = semaphore(phase, "a_setup_vector")
            q_ps = semaphore(phase, "a_q_psum")
            q_ev = semaphore(phase, "a_q_copied")
            q_sub = semaphore(phase, "a_q_less_max")
            q_exp = semaphore(phase, "a_q_exp")
            q_n = semaphore(phase, "a_q_normed")
            qt_ps = semaphore(phase, "a_qT_psum")
            qt_ok = semaphore(phase, "a_qT_copied")
            o_ps = semaphore(phase, "a_o_psum")
            o_ok = semaphore(phase, "a_o_ready")
            sq_ok = semaphore(phase, "a_o_squared")
            dv = semaphore(phase, "a_dve_order")

            @block.gpsimd
            def _(pool):
                flat = srci[:, 0:NG, :].rearrange("p g c -> p (g c)")

                def turn(first, half, count):
                    pool.wait_ge(pe_done, first + 1)
                    nc.gpsimd.tensor_copy(idxb[:, half, :], flat[:, bass.ds(first * 4, 16)]).then_inc(idx_ok, 1)
                    pool.wait_ge(idx_ok, count)
                    pool.sem_inc(turns, 1)
                    for s in range(16):
                        if s % 4 == 0 and s:
                            pool.wait_ge(pe_done, first + (s // 4 + 1))
                            pool.sem_inc(turns, 1)
                        nc.gpsimd.indirect_dma_start(
                            out=grows[:, s, :], out_offset=None, in_=table,
                            in_offset=bass.IndirectOffsetOnAxis(ap=idxb[:, half, s:s + 1], axis=0),
                        ).then_inc(got[s], 16)

                with nc.gpsimd.Fori(0, NG // 8) as i:
                    for half in range(2):
                        turn(i * 8 + 4 * half, half, i * 2 + (half + 1))
                turn(NG - 4, 0, NG // 4)

            @block.tensor
            def _(pe):
                pe.sem_inc(pe_done, 4)

                def aggregate(g, r, turn):
                    pe.wait_ge(s_ok, g + 1)
                    pe.wait_ge(acc_ok, g + 1)
                    for h in range(KC):
                        for c in range(GC):
                            if h == 0:
                                pe.wait_ge(got[4 * r + c], turn * 16 + 16)
                            last = nc.tensor.matmul(window(r % 2)[:, h, :], grows[:, 4 * r + c, h * P:(h + 1) * P],
                                                    S_t[:, r % 2, c, :], start=c == 0, stop=c == GC - 1)
                    last.then_inc(pe_done, 1)

                def group(i, base, off):
                    per, g0 = base
                    g = i * (4 * per) + (g0 + off)
                    return g, (g0 + off) % 4, i * per + (g0 + off) // 4

                def keys_values(t, u):
                    pe.wait_ge(zt_ok, t + 1)
                    pe.wait_ge(kv_ev, t + 1)
                    for k in range(KC):
                        last = nc.tensor.matmul(psA[u][:, 0:D], slot[:, u, k * P:(k + 1) * P], wqkv[:, k, P:3 * P],
                                                start=k == 0, stop=k == KC - 1)
                    last.then_inc(mm_ok, 1)

                for v_ in range(2):
                    aggregate(*group(0, (2, TA), v_))
                keys_values(0, 0)
                with nc.tensor.Fori(0, U) as i:
                    for u in range(UN):
                        aggregate(*group(i, (2, TA), 2 + 2 * u))
                        keys_values(i * UN + (u + 1), (u + 1) % 2)
                        aggregate(*group(i, (2, TA), 3 + 2 * u))

                pe.wait_ge(ks_ok, 1)
                nc.tensor.transpose(psT[:, 0:P], cn, ident[:, :]).then_inc(mid_pe, 1)
                pe.wait_ge(mid_dve, 1)
                last = nc.tensor.matmul(psO[0][:, 0:P], ones[:, :], cn, start=True, stop=True)
                last.then_inc(mid_pe, 1)
                pe.wait_ge(mem_ok, 1)
                nc.tensor.transpose(psO[1][0:MEM, 0:P], emk, ident[:, :])
                nc.tensor.transpose(psO[1][0:MEM, P:2 * P], mvv[:, :], ident[:, :]).then_inc(mid_pe, 1)
                pe.wait_ge(mid_dve, 2)
                nc.tensor.matmul(psC[:, 0:P + 1], emT[:, :], mvT[:, :], start=True, stop=False,
                                 skip_group_check=True)

                def context(t, u):
                    pe.wait_ge(ex_ok, t + 3)
                    nc.tensor.matmul(psC[:, 0:P + 1], esl[:, u, 0:P],
                                     kv[:, bass.ds(t, 1), P:2 * P + 1].rearrange("p a f -> p (a f)"),
                                     start=False, stop=False, skip_group_check=True).then_inc(cx_ok, 1)

                aggregate(*group(0, (1, TC), 0))
                context(0, 0)
                with nc.tensor.Fori(0, U) as i:
                    for u in range(UN):
                        aggregate(*group(i, (1, TC), 1 + u))
                        context(i * UN + (u + 1), (u + 1) % 2)

                pe.wait_ge(mid_dve, 3)
                nc.tensor.transpose(psT[:, 0:P], cn, ident[:, :]).then_inc(mid_pe, 1)
                pe.wait_ge(mid_dve, 4)
                nc.tensor.matmul(psO[0][:, 0:D], cnT, wout[:, :], start=True, stop=True).then_inc(mid_pe, 1)

                def queries(t, u):
                    pe.wait_ge(zt_ok, t + (T + 1))
                    for k in range(KC):
                        last = nc.tensor.matmul(psA[u][:, 0:P], slot[:, u, k * P:(k + 1) * P], wqkv[:, k, 0:P],
                                                start=k == 0, stop=k == KC - 1)
                    last.then_inc(q_ps, 1)

                def flip(t, u):
                    pe.wait_ge(q_n, t + 1)
                    nc.tensor.transpose(psT[:, 0:P], ksl[:, u, :], ident[:, :]).then_inc(qt_ps, 1)

                def attend(t, u):
                    pe.wait_ge(qt_ok, t + 1)
                    pe.wait_ge(o_ok, t + 1)
                    nc.tensor.matmul(psO[u][:, 0:D], qtl[:, u, :], cw[:, :], start=True, stop=True).then_inc(o_ps, 1)

                pe.wait_ge(mid_dve, 5)
                queries(0, 0)
                aggregate(*group(0, (1, TB), 0))
                with nc.tensor.Fori(0, U) as i:
                    for u in range(UN):
                        flip(i * UN + u, u % 2)
                        queries(i * UN + (u + 1), (u + 1) % 2)
                        aggregate(*group(i, (1, TB), 1 + u))
                        attend(i * UN + u, u % 2)
                flip(T - 1, 0)
                attend(T - 1, 0)

            @block.scalar
            def _(act):
                act.sem_inc(kv_ev, 2)
                act.sem_inc(cx_ok, 2)

                def z_copy(t, u):
                    act.activation(slot[:, u, :].rearrange("p (k n) -> p k n", k=KC), zT[:, :, bass.ds(t * P, P)],
                                   ACT.Copy).then_inc(zt_ok, 1)

                def kv_out(t, u):
                    act.wait_ge(mm_ok, t + 1)
                    act.activation(kv[:, bass.ds(t, 1), 0:2 * P].rearrange("p a f -> p (a f)"), psA[u][:, 0:D],
                                   ACT.Copy, scale=cq[:, bass.ds(t, 1)]).then_inc(kv_ev, 1)

                z_copy(0, 0)
                with nc.scalar.Fori(0, U) as i:
                    for u in range(UN):
                        z_copy(i * UN + (u + 1), (u + 1) % 2)
                        kv_out(i * UN + u, u % 2)
                kv_out(T - 1, 0)

                act.wait_ge(m_ok, 1)
                act.activation(emk, mk[:, :], ACT.Exp, bias=negM).then_inc(mem_ok, 1)

                def keys_exp(t, u):
                    act.wait_ge(ks_ok, t + 2)
                    act.wait_ge(cx_ok, t + 1)
                    act.activation(esl[:, u, 0:P], ksl[:, u, :], ACT.Exp).then_inc(ex_ok, 1)

                keys_exp(0, 0)
                with nc.scalar.Fori(0, U) as i:
                    for u in range(UN):
                        keys_exp(i * UN + (u + 1), (u + 1) % 2)

                def q_out(t, u):
                    act.wait_ge(q_ps, t + 1)
                    act.activation(qsl[:, u, :], psA[u][:, 0:P], ACT.Copy,
                                   scale=cq[:, bass.ds(t, 1)]).then_inc(q_ev, 1)

                def q_power(t, u):
                    act.wait_ge(q_sub, t + 1)
                    act.activation(qsl[:, u, :], qsl[:, u, :], ACT.Exp).then_inc(q_exp, 1)

                def qt_out(t, u):
                    act.wait_ge(qt_ps, t + 1)
                    act.activation(qtl[:, u, :], psT[:, 0:P], ACT.Copy).then_inc(qt_ok, 1)

                def square(t, u):
                    act.wait_ge(o_ok, t + 3)
                    act.activation(slotb[:, u, :], o_all[:, bass.ds(t, 1), :].rearrange("p a f -> p (a f)"),
                                   ACT.Square, accum_out=ssq[:, bass.ds(t, 1)]).then_inc(sq_ok, 1)
                    act.wait_ge(sq_ok, t + 1)

                z_copy(0, 0)
                q_out(0, 0)
                q_power(0, 0)
                with nc.scalar.Fori(0, U) as i:
                    for u in range(UN):
                        z_copy(i * UN + (u + 1), (u + 1) % 2)
                        qt_out(i * UN + u, u % 2)
                        q_out(i * UN + (u + 1), (u + 1) % 2)
                        q_power(i * UN + (u + 1), (u + 1) % 2)
                        square(i * UN + u, u % 2)
                qt_out(T - 1, 0)
                square(T - 1, 0)

            @block.vector
            def _(v):
                v.sem_inc(acc_ok, 2)
                v.sem_inc(ex_ok, 2)
                v.sem_inc(o_ok, 2)
                nc.vector.memset(kv[:, :, 2 * P:2 * P + 1], 1.0)
                nc.vector.memset(mvT[:, P:P + 1], 1.0)

                def onehots(g, r):
                    v.wait_ge(pe_done, g + 3)
                    nc.vector.tensor_tensor(
                        S_t[:, r % 2, :, :],
                        dstrel[:, bass.ds(g, 1), :].rearrange("p g c -> p (g c)").unsqueeze(2).to_broadcast([P, GC, WIN]),
                        iwin[:, 0:WIN].unsqueeze(1).to_broadcast([P, GC, WIN]), ALU.is_equal).then_inc(s_ok, 1)

                def add(g, r):
                    at = nc.vector.value_load(base_i[0:1, bass.ds(g, 1)], min_val=0, max_val=N)
                    v.wait_ge(pe_done, g + 5)
                    v.wait_ge(acc_ok, g + 2)
                    win = acc[:, :, bass.ds(at, WIN)]
                    nc.vector.tensor_tensor(win, win, window(r % 2), ALU.add).then_inc(acc_ok, 1)

                def group(i, base, off):
                    per, g0 = base
                    return i * (4 * per) + (g0 + off), (g0 + off) % 4

                def pair(i, base, off, between=None):
                    g, r = group(i, base, off)
                    onehots(g + 1, r + 1)
                    if between:
                        between()
                    add(g, r)

                onehots(0, 0)
                for n in range(2):
                    pair(0, (2, TA), n)
                with nc.vector.Fori(0, U) as i:
                    for n in range(2 * UN):
                        pair(i, (2, TA), 2 + n)

                ch = Chain(v, dv)
                v.wait_ge(kv_ev, T + 2)
                last = kv[:, T - 1, 0:P]
                ch.done(nc.vector.tensor_scalar(last, last, valid[:, :], negbig[:, :], ALU.mult, ALU.add))
                ch.done(nc.vector.tensor_reduce(cn, kv[:, :, 0:P].rearrange("p t c -> p c t"), AX.X, ALU.max))
                v.sem_inc(ks_ok, 1)
                v.wait_ge(mid_pe, 1)
                ch.done(nc.vector.tensor_reduce(small[:, 0:1], psT[:, 0:P], AX.X, ALU.max))
                ch.done(nc.vector.tensor_reduce(small[:, 2:3], mk[:, :], AX.X, ALU.max))
                ch.done(nc.vector.tensor_tensor(small[:, 0:1], small[:, 0:1], small[:, 2:3], ALU.max))
                ch.done(nc.vector.tensor_scalar(negM, small[:, 0:1], -1.0, None, ALU.mult))
                v.sem_inc(m_ok, 1)
                ch.done(nc.vector.tensor_scalar(cn, ident[:, :], small[:, 0:1], None, ALU.mult))
                v.sem_inc(mid_dve, 1)
                v.wait_ge(mid_pe, 2)
                ch.done(nc.vector.tensor_copy(mrow, psO[0][:, 0:P]))
                v.wait_ge(mid_pe, 3)
                ch.done(nc.vector.tensor_copy(emT[:, :], psO[1][0:MEM, 0:P]))
                ch.done(nc.vector.tensor_copy(mvT[:, 0:P], psO[1][0:MEM, P:2 * P]))
                v.sem_inc(mid_dve, 1)

                def keys_less_max(t, u):
                    v.wait_ge(ex_ok, t + 1)
                    nc.vector.tensor_tensor(ksl[:, u, :], kv[:, bass.ds(t, 1), 0:P].rearrange("p a f -> p (a f)"),
                                            mrow, ALU.subtract).then_inc(ks_ok, 1)

                pair(0, (1, TC), 0, lambda: keys_less_max(0, 0))
                with nc.vector.Fori(0, U) as i:
                    for u in range(UN):
                        pair(i, (1, TC), 1 + u, lambda: keys_less_max(i * UN + (u + 1), (u + 1) % 2))

                v.wait_ge(cx_ok, T + 2)
                ch.done(nc.vector.reciprocal(small[:, 3:4], psC[:, P:P + 1]))
                ch.done(nc.vector.tensor_scalar(cn, psC[:, 0:P], small[:, 3:4], float(DH) ** -0.5, ALU.mult,
                                                ALU.mult))
                ch.done(nc.vector.tensor_tensor(cn, cn, bmask[:, :], ALU.mult))
                v.sem_inc(mid_dve, 1)
                v.wait_ge(mid_pe, 4)
                ch.done(nc.vector.tensor_copy(cnT, psT[:, 0:P]))
                v.sem_inc(mid_dve, 1)
                v.wait_ge(mid_pe, 5)
                ch.done(nc.vector.tensor_copy(cw[:, :], psO[0][:, 0:D]))
                v.sem_inc(mid_dve, 1)

                def heads(ap):
                    return ap.rearrange("p (h d) -> p h d", h=HEADS)

                def query_norm(t, u, link):
                    v.wait_ge(q_ev, t + 1)
                    q, top, tot = qsl[:, u, :], small[:, 8:12], small[:, 12:16]
                    link.done(nc.vector.tensor_reduce(top, heads(q), AX.X, ALU.max))
                    nc.vector.tensor_tensor(heads(q), heads(q), top.unsqueeze(2).to_broadcast([P, HEADS, DH]),
                                            ALU.subtract).then_inc(q_sub, 1)
                    v.wait_ge(q_exp, t + 1)
                    link.done(nc.vector.tensor_reduce(tot, heads(q), AX.X, ALU.add))
                    link.done(nc.vector.reciprocal(tot, tot))
                    nc.vector.tensor_tensor(heads(ksl[:, u, :]), heads(q),
                                            tot.unsqueeze(2).to_broadcast([P, HEADS, DH]), ALU.mult).then_inc(q_n, 1)

                def out_row(t, u):
                    v.wait_ge(o_ps, t + 1)
                    nc.vector.tensor_tensor(o_all[:, bass.ds(t, 1), :].rearrange("p a f -> p (a f)"),
                                            psO[u][:, 0:D], bout[:, :], ALU.add).then_inc(o_ok, 1)

                LINKS = 3
                pair(0, (1, TB), 0, lambda: query_norm(0, 0, ch))
                start = ch.n
                with nc.vector.Fori(0, U) as i:
                    for u in range(UN):
                        link = Chain(v, dv, i * (UN * LINKS) + (start + u * LINKS))
                        pair(i, (1, TB), 1 + u, lambda: query_norm(i * UN + (u + 1), (u + 1) % 2, link))
                        out_row(i * UN + u, u % 2)
                out_row(T - 1, 0)
                v.wait_ge(acc_ok, NG + 2)

        over(phase)

        phase = []
        with nc.Block() as block:
            rows_in = [semaphore(phase, f"s_rows{k}") for k in range(GC)]
            idx_ok = semaphore(phase, "s_indices")
            turns = semaphore(phase, "s_turns")
            hot_ok = semaphore(phase, "s_onehots")
            prod_ok = semaphore(phase, "s_products")
            sum_ok = semaphore(phase, "s_added")
            dv = semaphore(phase, "s_dve_order")
            dcur = small[:, 16:16 + GC]

            @block.gpsimd
            def _(pool):
                flag = nc.gpsimd.value_load(flag_i[0:1, 0:1], min_val=0, max_val=1)
                with nc.gpsimd.If(flag > 0):
                    with nc.gpsimd.Fori(0, NG) as g:
                        pool.wait_ge(sum_ok, g * SW + 1)
                        nc.gpsimd.tensor_copy(idxb[:, 0, 0:GC], srci[:, bass.ds(g, 1), :].rearrange("p g c -> p (g c)"))\
                            .then_inc(idx_ok, 1)
                        pool.wait_ge(idx_ok, g + 1)
                        pool.sem_inc(turns, 1)
                        for c in range(GC):
                            nc.gpsimd.indirect_dma_start(
                                out=grows[:, c, :], out_offset=None, in_=table,
                                in_offset=bass.IndirectOffsetOnAxis(ap=idxb[:, 0, c:c + 1], axis=0),
                            ).then_inc(rows_in[c], 16)
                        for c in range(GC):
                            pool.wait_ge(rows_in[c], g * 16 + 16)

            @block.tensor
            def _(pe):
                flag = nc.tensor.value_load(flag_i[0:1, 0:1], min_val=0, max_val=1)
                with nc.tensor.If(flag > 0):
                    with nc.tensor.Fori(0, NG) as g:
                        for c in range(GC):
                            pe.wait_ge(rows_in[c], g * 16 + 16)
                        for c in range(GC):
                            pe.wait_ge(rows_in[c], g * 16 + 16)
                        pe.sem_inc(turns, 1)
                        with nc.tensor.Fori(0, SW) as w:
                            pe.wait_ge(hot_ok, g * SW + w + 1)
                            for h in range(KC):
                                for c in range(GC):
                                    last = nc.tensor.matmul(window(2)[:, h, :], grows[:, c, h * P:(h + 1) * P],
                                                            S_t[:, 0, c, :], start=c == 0, stop=c == GC - 1)
                            last.then_inc(prod_ok, 1)

            @block.vector
            def _(v):
                v.sem_inc(sum_ok, 1)
                flag = nc.vector.value_load(flag_i[0:1, 0:1], min_val=0, max_val=1)
                with nc.vector.If(flag > 0):
                    with nc.vector.Fori(0, NG) as g:
                        nc.vector.tensor_copy(dcur, dslow[:, bass.ds(g, 1), :].rearrange("p g c -> p (g c)"))\
                            .then_inc(dv, 1)
                        v.wait_ge(dv, g * (2 * SW + 1) + 1)
                        v.sem_inc(turns, 1)
                        with nc.vector.Fori(0, SW) as w:
                            nc.vector.tensor_tensor(S_t[:, 0, :, :], dcur.unsqueeze(2).to_broadcast([P, GC, WIN]),
                                                    iwin[:, 0:WIN].unsqueeze(1).to_broadcast([P, GC, WIN]),
                                                    ALU.is_equal).then_inc(hot_ok, 1)
                            v.wait_ge(hot_ok, g * SW + w + 1)
                            nc.vector.tensor_scalar(dcur, dcur, float(-WIN), None, ALU.add).then_inc(dv, 1)
                            v.wait_ge(prod_ok, g * SW + w + 1)
                            win = acc[:, :, bass.ds(w * WIN, WIN)]
                            nc.vector.tensor_tensor(win, win, window(2), ALU.add).then_inc(dv, 1)
                            v.wait_ge(dv, g * (2 * SW + 1) + w * 2 + 3)
                            v.sem_inc(sum_ok, 1)

        over(phase)

        aw, bw, a1 = gw[:, 0, :], gw[:, 1, :], small[:, 20:21]
        tot2 = small[:, 24:26]
        rs = cq

        phase = []
        with nc.Block() as block:
            xs_in = [semaphore(phase, f"c_x{k}") for k in range(4)]
            at_ok = semaphore(phase, "c_tile_copied")
            pr_ok = semaphore(phase, "c_products")
            y_ok = semaphore(phase, "c_rows_ready")
            xb_ok = semaphore(phase, "c_x_plus_norm")
            on_ok = semaphore(phase, "c_attention_normed")
            res_ok = semaphore(phase, "c_residual_summed")
            root_in = semaphore(phase, "c_root_in")
            root_ok = semaphore(phase, "c_root_done")
            dv = semaphore(phase, "c_dve_order")
            part = semaphore(phase, "c_partial_sums")
            whole = semaphore(phase, "c_total_sums")

            @block.sync
            def _(sp):
                def x_tile(t, u, rows=P):
                    sp.wait_ge(res_ok, t + 1)
                    src_ = a_x[bass.ds(t * P, P), :] if rows == P else a_x[(T - 1) * P:N, :]
                    sp.dma_start(grows[0:rows, u, :], src_).then_inc(xs_in[u], 16)

                with nc.sync.Fori(0, U) as i:
                    for u in range(UN):
                        x_tile(i * UN + u, u)
                x_tile(T - 1, 0, TAIL)

            @block.scalar
            def _(act):
                act.wait_ge(root_in, 1)
                act.activation(sa[:, :], sc[:, :], ACT.Sqrt).then_inc(root_ok, 1)

                def tile(t, u, turn):
                    act.wait_ge(pr_ok, t + 1)
                    act.activation(slot[:, u, :].rearrange("p (k n) -> p k n", k=KC), acc[:, :, bass.ds(t * P, P)],
                                   ACT.Copy).then_inc(at_ok, 1)
                    act.wait_ge(xs_in[u], turn * 16 + 16)
                    act.activation(grows[:, u, :], grows[:, u, :], ACT.Identity, scale=x1s[:, bass.ds(t, 1)],
                                   bias=x1b[:, bass.ds(t, 1)]).then_inc(xb_ok, 1)

                with nc.scalar.Fori(0, U) as i:
                    for u in range(UN):
                        tile(i * UN + u, u, i)
                tile(T - 1, 0, U)
                act.wait_ge(root_in, 2)
                act.activation(small[:, 30:31], small[:, 31:32], ACT.Sqrt).then_inc(root_ok, 1)

            @block.tensor
            def _(pe):
                pe.sem_inc(pr_ok, 4)

                def tile(t, u):
                    pe.wait_ge(at_ok, t + 1)
                    pe.wait_ge(y_ok, t + 1)
                    for k in range(KC):
                        last = nc.tensor.matmul(ps[u % 2][:, 0:D], slot[:, u, k * P:(k + 1) * P], gw[:, k, :],
                                                start=k == 0, stop=k == KC - 1)
                    last.then_inc(pr_ok, 1)

                with nc.tensor.Fori(0, U) as i:
                    for u in range(UN):
                        tile(i * UN + u, u)
                tile(T - 1, 0)
                for n in range(2):
                    pe.wait_ge(part, n + 1)
                    nc.tensor.matmul(ps[2][:, n:n + 1], ones[:, :], small[:, 24 + n:25 + n], start=True,
                                     stop=True).then_inc(whole, 1)

            @block.gpsimd
            def _(pool):
                pool.sem_inc(res_ok, 4)

                def tile(t, u):
                    pool.wait_ge(xb_ok, t + 1)
                    pool.wait_ge(on_ok, t + 1)
                    row = o_all[:, bass.ds(t, 1), :].rearrange("p a f -> p (a f)")
                    nc.gpsimd.tensor_tensor(row, row, grows[:, u, :], ALU.add).then_inc(res_ok, 1)

                with nc.gpsimd.Fori(0, U) as i:
                    for u in range(UN):
                        tile(i * UN + u, u)
                tile(T - 1, 0)

            @block.vector
            def _(v):
                v.sem_inc(y_ok, 2)
                ch = Chain(v, dv)
                ch.done(nc.vector.tensor_scalar(sc[:, :], ssq[:, :], 1e-24, None, ALU.max))
                v.sem_inc(root_in, 1)
                v.wait_ge(root_ok, 1)
                ch.done(nc.vector.reciprocal(rs[:, :], sa[:, :]))
                ch.done(nc.vector.tensor_tensor(sd[:, :], rs[:, :], rs[:, :], ALU.mult))
                ch.done(nc.vector.tensor_tensor(sd[:, :], sd[:, :], sc[:, :], ALU.mult))
                ch.done(nc.vector.tensor_scalar(sd[:, :], sd[:, :], -0.5, 1.5, ALU.mult, ALU.add))
                ch.done(nc.vector.scalar_tensor_tensor(rs[:, :], rs[:, :], float(D) ** 0.5, sd[:, :], ALU.mult,
                                                       ALU.mult))

                def tile(t, u):
                    v.wait_ge(pr_ok, t + 5)
                    row = y_all[:, bass.ds(t, 1), :].rearrange("p a f -> p (a f)")
                    nc.vector.scalar_tensor_tensor(row, ps[u % 2][:, 0:D], dinv[:, bass.ds(t, 1)], cbias[:, :],
                                                   ALU.mult, ALU.add).then_inc(y_ok, 1)
                    o = o_all[:, bass.ds(t, 1), :].rearrange("p a f -> p (a f)")
                    nc.vector.scalar_tensor_tensor(o, o, rs[:, bass.ds(t, 1)], gout[:, :], ALU.mult,
                                                   ALU.mult).then_inc(on_ok, 1)
                    v.wait_ge(y_ok, t + 3)
                    return nc.vector.bn_stats(stats[:, bass.ds(t, 1), :].rearrange("p a f -> p (a f)"), row)

                with nc.vector.Fori(0, U) as i:
                    for u in range(UN):
                        tile(i * UN + u, u)
                ch.done(tile(T - 1, 0))
                most, full = float((T - 1) * D), 1.0 / (N * D)
                pm, tm = small[:, 32:34], small[:, 34:36]
                ch.done(nc.vector.bn_aggr(pm, stats[:, 0:T - 1, :].rearrange("p t s -> p (t s)")))
                ch.done(nc.vector.bn_aggr(tm, stats[:, T - 1, :]))
                ch.done(nc.vector.tensor_scalar(tm[:, 0:1], tm[:, 0:1], valid[:, :], float(D), ALU.mult, ALU.mult))
                ch.done(nc.vector.scalar_tensor_tensor(tot2[:, 0:1], pm[:, 0:1], most, tm[:, 0:1], ALU.mult, ALU.add))
                v.sem_inc(part, 1)
                ch.done(nc.vector.tensor_scalar(tm[:, 0:1], tm[:, 0:1], 1.0 / D, None, ALU.mult))
                v.wait_ge(whole, 1)
                mu = small[:, 36:37]
                ch.done(nc.vector.tensor_scalar(mu, ps[2][:, 0:1], full, None, ALU.mult))
                d1, d2 = small[:, 37:38], small[:, 38:39]
                ch.done(nc.vector.tensor_tensor(d1, pm[:, 0:1], mu, ALU.subtract))
                ch.done(nc.vector.tensor_tensor(d1, d1, d1, ALU.mult))
                ch.done(nc.vector.tensor_tensor(d1, d1, pm[:, 1:2], ALU.add))
                ch.done(nc.vector.tensor_tensor(d2, tm[:, 0:1], mu, ALU.subtract))
                ch.done(nc.vector.tensor_tensor(d2, d2, d2, ALU.mult))
                ch.done(nc.vector.tensor_tensor(d2, d2, tm[:, 1:2], ALU.add))
                ch.done(nc.vector.tensor_scalar(d2, d2, valid[:, :], float(D), ALU.mult, ALU.mult))
                ch.done(nc.vector.scalar_tensor_tensor(tot2[:, 1:2], d1, most, d2, ALU.mult, ALU.add))
                v.sem_inc(part, 1)
                v.wait_ge(whole, 2)
                val, root = small[:, 31:32], small[:, 30:31]
                ch.done(nc.vector.tensor_scalar(val, ps[2][:, 1:2], full, 1e-30, ALU.mult, ALU.max))
                v.sem_inc(root_in, 1)
                v.wait_ge(root_ok, 2)
                ch.done(nc.vector.reciprocal(d1, root))
                ch.done(nc.vector.tensor_tensor(d1, d1, val, ALU.mult))
                ch.done(nc.vector.tensor_tensor(d1, d1, root, ALU.add))
                ch.done(nc.vector.tensor_scalar(d1, d1, 0.5, EPS, ALU.mult, ALU.add))
                ch.done(nc.vector.reciprocal(d2, d1))
                ch.done(nc.vector.tensor_scalar(aw, lnw[:, :], d2, None, ALU.mult))
                ch.done(nc.vector.tensor_scalar(bw, aw, mu, None, ALU.mult))
                ch.done(nc.vector.tensor_tensor(bw, lnb[:, :], bw, ALU.subtract))
                ch.done(nc.vector.tensor_scalar(a1, pre[:, :], -1.0, 1.0, ALU.mult, ALU.add))

        over(phase)

        w2_sb = R3[:, 0:NX * HC * D].rearrange("p (e h f) -> p e h f", e=NX, h=HC)
        room = NX * HC * D

        def lanes(k):
            return R3[:, room + k * T * NX:room + (k + 1) * T * NX].rearrange("p (t e) -> p t e", e=NX)

        L, M1, M2, MM, LA, LB, LC, LD = (lanes(k) for k in range(8))
        rt = R3[:, room + 8 * T * NX:]
        top, sec, w1c, w2c = rt[:, 0:T], rt[:, T:2 * T], x1s, x1b
        r8, eb = rt[:, 2 * T:2 * T + NX], rt[:, 2 * T + NX:2 * T + 2 * NX]
        tl, cumt = rt[:, 2 * T + 2 * NX:2 * T + 3 * NX], rt[:, 2 * T + 3 * NX:2 * T + 4 * NX]
        cnt = rt[:, 2 * T + 5 * NX:2 * T + 6 * NX]
        mask, eidf = (rt[:, 160 + 128 * k:160 + 128 * k + NSTEP] for k in range(2))
        flat = S_t[:, :, :, :].rearrange("p s c w -> p (s c w)")
        ints = flat.bitcast(i32)
        gat, sct, eid_i = ints[:, 0:NTILE], ints[:, NTILE:2 * NTILE], ints[0:1, 2 * NTILE:2 * NTILE + NSTEP]
        tag_i, dump_i = ints[:, 320:320 + 2 * T], ints[:, 320 + 2 * T:320 + 2 * T + NTILE]
        tag = flat[:, 530:530 + 2 * T]
        dump = flat[:, 640:640 + NTILE]
        posf, hif, lof = (rt[:, 500 + 100 * k:500 + 100 * k + 2 * T] for k in range(3))
        pos_i, part_i = (rt[:, 800 + 100 * k:800 + 100 * k + 2 * T].bitcast(i32) for k in range(2))
        pad = rt[:, 1000:1000 + NTILE]
        held = rt[:, 1110:1110 + NTILE]
        held_i = rt[:, 1220:1220 + NTILE].bitcast(i32)
        lo1 = [R2[:, n * IB * P:(n + 1) * IB * P].rearrange("p (c j) -> p c j", c=IB) for n in range(2)]
        hi1 = [R2[:, 2 * IB * P + n * IB * NTILE:2 * IB * P + (n + 1) * IB * NTILE]
               .rearrange("p (c j) -> p c j", c=IB) for n in range(2)]
        uT = [grows[:, 4 + k, :] for k in range(2)]
        zero_c = grows[:, 6, 0:P]

        phase = []
        with nc.Block() as block:
            w2_in = semaphore(phase, "r_w2_in")
            y1 = semaphore(phase, "r_scaled")
            y2 = semaphore(phase, "r_shifted")
            ng_ok = semaphore(phase, "r_negative_part")
            xa_ok = semaphore(phase, "r_residual_added")
            x_ok = semaphore(phase, "r_x1_ready")
            st_ok = semaphore(phase, "r_stats")
            root_in = semaphore(phase, "r_root_in")
            root_ok = semaphore(phase, "r_root_done")
            dv = semaphore(phase, "r_dve_order")
            aff = semaphore(phase, "r_affine")
            n_ok = semaphore(phase, "r_n_ready")
            keep = [semaphore(phase, f"r_n_kept{k}") for k in range(4)]
            f_ps = semaphore(phase, "r_nT_psum")
            f_ok = semaphore(phase, "r_nT_ready")
            l_ps = semaphore(phase, "r_logits_psum")
            l_ok = semaphore(phase, "r_logits")
            ex_in = semaphore(phase, "r_exp_in")
            ex_ok = semaphore(phase, "r_exp_done")
            hot = semaphore(phase, "r_choices")
            rank = semaphore(phase, "r_ranks_psum")
            placed = semaphore(phase, "r_places")
            pl = semaphore(phase, "r_pool_order")
            tags = semaphore(phase, "r_tags")
            pl_hot = semaphore(phase, "r_place_onehots")
            pl_tag = semaphore(phase, "r_place_onehots_tagged")
            pl_free = semaphore(phase, "r_place_onehots_free")
            inv_ok = semaphore(phase, "r_inverse_psum")

            @block.sync
            def _(sp):
                sp.dma_start(R3[:, 0:room], a_w2).then_inc(w2_in, 16)

                def keep_tile(t, u):
                    sp.wait_ge(n_ok, t + 1)
                    sp.dma_start(table[bass.ds(t * P, P), :], slot[:, u, :]).then_inc(keep[u], 16)

                with nc.sync.Fori(0, U) as i:
                    for u in range(UN):
                        keep_tile(i * UN + u, u)
                sp.wait_ge(n_ok, T)
                sp.dma_start(table[(T - 1) * P:N, :], slot[0:TAIL, 0, :]).then_inc(keep[0], 16)
                for u in range(UN):
                    sp.wait_ge(keep[u], 16 * (U + (1 if u == 0 else 0)))
                sp.wait_ge(w2_in, 16)

            @block.scalar
            def _(act):
                def negative(t, u):
                    act.wait_ge(y2, t + 1)
                    act.activation(slotb[:, u % 2, :], slot[:, 2 + u % 2, :], ACT.Relu, scale=-1.0).then_inc(ng_ok, 1)

                with nc.scalar.Fori(0, U) as i:
                    for u in range(UN):
                        negative(i * UN + u, u)
                negative(T - 1, 0)
                for n in range(2):
                    act.wait_ge(root_in, n + 1)
                    act.activation(sa[:, :], sc[:, :], ACT.Sqrt).then_inc(root_ok, 1)
                act.wait_ge(aff, 1)

                def norm(t, u, turn):
                    act.wait_ge(keep[u], turn * 16)
                    act.wait_ge(f_ps, t + 1)
                    act.activation(slot[:, u, :], o_all[:, bass.ds(t, 1), :].rearrange("p a f -> p (a f)"),
                                   ACT.Identity, scale=zs_s[:, bass.ds(t, 1)],
                                   bias=zs_b[:, bass.ds(t, 1)]).then_inc(n_ok, 1)

                act.sem_inc(f_ps, 4)
                with nc.scalar.Fori(0, U) as i:
                    for u in range(UN):
                        norm(i * UN + u, u, i)
                norm(T - 1, 0, U)
                act.wait_ge(ex_in, 1)
                act.activation(w2c[:, :], sec, ACT.Exp).then_inc(ex_ok, 1)

            @block.gpsimd
            def _(pool):
                def residual(t, u):
                    pool.wait_ge(y2, t + 1)
                    row = o_all[:, bass.ds(t, 1), :].rearrange("p a f -> p (a f)")
                    nc.gpsimd.tensor_tensor(row, row, slot[:, 2 + u % 2, :], ALU.add).then_inc(xa_ok, 1)

                with nc.gpsimd.Fori(0, U) as i:
                    for u in range(UN):
                        residual(i * UN + u, u)
                residual(T - 1, 0)
                nc.gpsimd.iota(tag_i, pattern=[[2 * P, T], [1, 2]], base=1, channel_multiplier=2).then_inc(pl, 1)
                nc.gpsimd.iota(dump_i, pattern=[[P, NTILE]], base=2 * N + 1, channel_multiplier=1).then_inc(pl, 1)
                pool.wait_ge(pl, 2)
                nc.gpsimd.tensor_copy(tag, tag_i).then_inc(tags, 1)
                nc.gpsimd.tensor_copy(dump, dump_i).then_inc(tags, 1)
                pool.wait_ge(tags, 2)
                with nc.gpsimd.Fori(0, T // IB) as i:
                    for n in range(2):
                        m = i * 2 + n
                        pool.wait_ge(pl_hot, m + 1)
                        nc.gpsimd.tensor_tensor(hi1[n], hi1[n], tag[:, bass.ds(m * IB, IB)].unsqueeze(2)
                                                .to_broadcast([P, IB, NTILE]), ALU.mult).then_inc(pl_tag, 1)

            @block.tensor
            def _(pe):
                def flip(t, u):
                    pe.wait_ge(n_ok, t + 1)
                    pe.wait_ge(f_ok, t + 1)
                    for k in range(KC):
                        last = nc.tensor.transpose(ps[u % 2][:, k * P:(k + 1) * P], slot[:, u, k * P:(k + 1) * P],
                                                   ident[:, :])
                    last.then_inc(f_ps, 1)

                def logits(t, u):
                    pe.wait_ge(f_ok, t + 3)
                    pe.wait_ge(l_ok, t + 1)
                    for k in range(KC):
                        last = nc.tensor.matmul(ps[2 + u % 2][:, 0:NX], uT[u % 2][:, k * P:(k + 1) * P], wr[:, k, :],
                                                start=k == 0, stop=k == KC - 1)
                    last.then_inc(l_ps, 1)

                flip(0, 0)
                with nc.tensor.Fori(0, U) as i:
                    for u in range(UN):
                        flip(i * UN + (u + 1), (u + 1) % UN)
                        logits(i * UN + u, u)
                logits(T - 1, 0)
                pe.wait_ge(hot, 1)
                nc.tensor.matmul(ps[4][:, 0:T * NX], tri[:, :], MM.rearrange("p t e -> p (t e)"), start=True, stop=True)
                nc.tensor.matmul(ps[5][:, 0:T * NX], ones[:, :], MM.rearrange("p t e -> p (t e)"), start=True,
                                 stop=True).then_inc(rank, 1)
                pe.sem_inc(pl_free, 2)
                nc.tensor.matmul(ps[6][:, 0:NTILE], zero_c, zero_c[:, 0:NTILE], start=True, stop=False)
                with nc.tensor.Fori(0, T // IB) as i:
                    for n in range(2):
                        pe.wait_ge(pl_tag, i * 2 + (n + 1))
                        for c in range(IB):
                            last = nc.tensor.matmul(ps[6][:, 0:NTILE], lo1[n][:, c, :], hi1[n][:, c, :],
                                                    start=False, stop=False)
                        last.then_inc(pl_free, 1)
                nc.tensor.matmul(ps[6][:, 0:NTILE], zero_c, zero_c[:, 0:NTILE], start=False,
                                 stop=True).then_inc(inv_ok, 1)

            @block.vector
            def _(v):
                nc.vector.memset(zero_c, 0.0)
                v.sem_inc(x_ok, 2)
                v.sem_inc(f_ok, 2)
                v.sem_inc(l_ok, 2)

                def scale_shift(t, u):
                    nc.vector.tensor_tensor(slot[:, u % 2, :], y_all[:, bass.ds(t, 1), :].rearrange("p a f -> p (a f)"),
                                            aw, ALU.mult).then_inc(y1, 1)
                    v.wait_ge(y1, t + 1)
                    if not (isinstance(t, int) and t < 2):
                        v.wait_ge(xa_ok, t - 1)
                    nc.vector.tensor_tensor(slot[:, 2 + u % 2, :], slot[:, u % 2, :], bw, ALU.add).then_inc(y2, 1)

                def finish(t, u):
                    v.wait_ge(ng_ok, t + 1)
                    v.wait_ge(xa_ok, t + 1)
                    row = o_all[:, bass.ds(t, 1), :].rearrange("p a f -> p (a f)")
                    nc.vector.scalar_tensor_tensor(row, slotb[:, u % 2, :], a1, row, ALU.mult, ALU.add).then_inc(x_ok, 1)
                    v.wait_ge(x_ok, t + 3)
                    nc.vector.bn_stats(stats[:, bass.ds(t, 1), :].rearrange("p a f -> p (a f)"), row).then_inc(st_ok, 1)

                scale_shift(0, 0)
                scale_shift(1, 1)
                finish(0, 0)
                with nc.vector.Fori(0, U - 1) as i:
                    for u in range(UN):
                        scale_shift(i * UN + (u + 2), u % 2)
                        finish(i * UN + (u + 1), (u + 1) % 2)
                for t in range((U - 1) * UN + 2, T):
                    scale_shift(t, t % 2)
                    finish(t - 1, (t - 1) % 2)
                finish(T - 1, (T - 1) % 2)
                v.wait_ge(st_ok, T)
                ch = Chain(v, dv)
                for t in range(T):
                    last = nc.vector.bn_aggr(mv[:, t, :], stats[:, t, :])
                ch.done(last)
                mean, var = mv[:, :, 0], mv[:, :, 1]

                def rsqrt(out, val, count):
                    v.sem_inc(root_in, 1)
                    v.wait_ge(root_ok, count)
                    ch.done(nc.vector.reciprocal(out, sa[:, :]))
                    ch.done(nc.vector.tensor_tensor(sd[:, :], out, out, ALU.mult))
                    ch.done(nc.vector.tensor_tensor(sd[:, :], sd[:, :], val, ALU.mult))
                    ch.done(nc.vector.tensor_scalar(sd[:, :], sd[:, :], -0.5, 1.5, ALU.mult, ALU.add))
                    ch.done(nc.vector.tensor_tensor(out, out, sd[:, :], ALU.mult))

                ch.done(nc.vector.tensor_scalar(sc[:, :], var, EPS, None, ALU.add))
                rsqrt(zs_s[:, :], sc[:, :], 1)
                ch.done(nc.vector.tensor_tensor(sc[:, :], zs_s[:, :], zs_s[:, :], ALU.mult))
                ch.done(nc.vector.tensor_tensor(sc[:, :], sc[:, :], var, ALU.mult))
                ch.done(nc.vector.tensor_scalar(sc[:, :], sc[:, :], EPS, None, ALU.add))
                rsqrt(rstd[:, :], sc[:, :], 2)
                ch.done(nc.vector.tensor_tensor(zs_s[:, :], zs_s[:, :], rstd[:, :], ALU.mult))
                ch.done(nc.vector.scalar_tensor_tensor(zs_b[:, :], mean, -1.0, zs_s[:, :], ALU.mult, ALU.mult))
                v.sem_inc(aff, 1)

                def widen(t, u):
                    v.wait_ge(f_ps, t + 5)
                    for k in range(KC):
                        last = nc.vector.tensor_scalar(uT[u % 2][:, k * P:(k + 1) * P], ps[u % 2][:, k * P:(k + 1) * P],
                                                       gamma[:, k:k + 1], beta[:, k:k + 1], ALU.mult, ALU.add)
                    last.then_inc(f_ok, 1)

                def collect(t, u):
                    v.wait_ge(l_ps, t + 1)
                    nc.vector.tensor_tensor(L[:, bass.ds(t, 1), :].rearrange("p a f -> p (a f)"),
                                            ps[2 + u % 2][:, 0:NX], brr[:, :], ALU.add).then_inc(l_ok, 1)

                widen(0, 0)
                with nc.vector.Fori(0, U) as i:
                    for u in range(UN):
                        widen(i * UN + (u + 1), (u + 1) % 2)
                        collect(i * UN + u, u % 2)
                collect(T - 1, 0)
                v.wait_ge(l_ok, T + 2)

                shape = [P, T, NX]

                def over_e(ap):
                    return ap.unsqueeze(2).to_broadcast(shape)

                ch.done(nc.vector.tensor_scalar(r8, iwin[:, 0:NX], -1.0, float(NX), ALU.mult, ALU.add))

                def choose(out, logit, peak, tmp):
                    ch.done(nc.vector.tensor_reduce(peak, logit, AX.X, ALU.max))
                    ch.done(nc.vector.tensor_tensor(tmp, logit, over_e(peak), ALU.is_equal))
                    ch.done(nc.vector.tensor_tensor(tmp, tmp, r8.unsqueeze(1).to_broadcast(shape), ALU.mult))
                    ch.done(nc.vector.tensor_reduce(mask[:, 0:T], tmp, AX.X, ALU.max))
                    ch.done(nc.vector.tensor_tensor(out, tmp, over_e(mask[:, 0:T]), ALU.is_equal))

                choose(M1, L, top, LA)
                ch.done(nc.vector.scalar_tensor_tensor(LB, M1, -1e30, L, ALU.mult, ALU.add))
                choose(M2, LB, sec, LA)
                ch.done(nc.vector.tensor_tensor(MM, M1, M2, ALU.add))
                ch.done(nc.vector.tensor_scalar(MM[:, T - 1, :], MM[:, T - 1, :], valid[:, :], None, ALU.mult))
                v.sem_inc(hot, 1)
                ch.done(nc.vector.tensor_tensor(sec, sec, top, ALU.subtract))
                v.sem_inc(ex_in, 1)
                v.wait_ge(ex_ok, 1)
                ch.done(nc.vector.tensor_scalar(w1c[:, :], w2c[:, :], 1.0, None, ALU.add))
                ch.done(nc.vector.reciprocal(w1c[:, :], w1c[:, :]))
                ch.done(nc.vector.tensor_tensor(w2c[:, :], w2c[:, :], w1c[:, :], ALU.mult))
                v.wait_ge(rank, 1)
                total = ps[5][:, 0:T * NX].rearrange("p (t e) -> p t e", e=NX)
                within = ps[4][:, 0:T * NX].rearrange("p (t e) -> p t e", e=NX)
                ch.done(nc.vector.tensor_copy(LA, total))
                a, b, s = LA, LB, 1
                while s < T:
                    nc.vector.tensor_copy(b[:, 0:s, :], a[:, 0:s, :])
                    ch.done(nc.vector.tensor_tensor(b[:, s:T, :], a[:, s:T, :], a[:, 0:T - s, :], ALU.add))
                    a, b, s = b, a, 2 * s
                ch.done(nc.vector.tensor_copy(cnt, a[:, T - 1, :]))
                ch.done(nc.vector.tensor_scalar(mask[:, 0:T], iwin[:, 0:T], float(P), None, ALU.mult))
                ev = LD.rearrange("p t e -> p (t e)").rearrange("p (e t) -> p e t", e=NX)
                ch.done(nc.vector.tensor_tensor(ev, cnt.unsqueeze(2).to_broadcast([P, NX, T]),
                                                mask[:, 0:T].unsqueeze(1).to_broadcast([P, NX, T]), ALU.is_gt))
                ch.done(nc.vector.tensor_reduce(tl, ev, AX.X, ALU.add))
                ch.done(nc.vector.tensor_copy(cumt, tl))
                for e in range(1, NX):
                    ch.done(nc.vector.tensor_tensor(cumt[:, e:e + 1], cumt[:, e:e + 1], cumt[:, e - 1:e], ALU.add))
                ch.done(nc.vector.tensor_tensor(eb, cumt, tl, ALU.subtract))
                ch.done(nc.vector.tensor_scalar(eb, eb, float(P), None, ALU.mult))
                ch.done(nc.vector.tensor_tensor(LC, a, total, ALU.subtract))
                ch.done(nc.vector.tensor_tensor(LC, LC, within, ALU.add))
                ch.done(nc.vector.tensor_tensor(LC, LC, eb.unsqueeze(1).to_broadcast(shape), ALU.add))
                pk = posf.rearrange("p (t k) -> p t k", k=2)
                for k, m in ((0, M1), (1, M2)):
                    ch.done(nc.vector.tensor_tensor(LD, LC, m, ALU.mult))
                    ch.done(nc.vector.tensor_reduce(pk[:, :, k], LD, AX.X, ALU.add))
                ch.done(nc.vector.tensor_copy(pos_i, posf))
                ch.done(nc.vector.tensor_scalar(part_i, pos_i, 7, None, ALU.arith_shift_right))
                ch.done(nc.vector.tensor_copy(hif, part_i))
                ch.done(nc.vector.tensor_scalar(part_i, pos_i, P - 1, None, ALU.bitwise_and))
                ch.done(nc.vector.tensor_copy(lof, part_i))
                late = hif[:, 2 * T - 2:2 * T]
                ch.done(nc.vector.tensor_scalar(late, late, 1.0, valid[:, :], ALU.add, ALU.mult))
                ch.done(nc.vector.tensor_scalar(late, late, -1.0, None, ALU.add))
                with nc.vector.Fori(0, T // IB) as i:
                    for n in range(2):
                        m = i * 2 + n
                        v.wait_ge(pl_free, m + 1)
                        nc.vector.tensor_tensor(hi1[n], hif[:, bass.ds(m * IB, IB)].unsqueeze(2)
                                                .to_broadcast([P, IB, NTILE]), iwin[:, 0:NTILE].unsqueeze(1)
                                                .to_broadcast([P, IB, NTILE]), ALU.is_equal)
                        nc.vector.tensor_tensor(lo1[n], lof[:, bass.ds(m * IB, IB)].unsqueeze(2)
                                                .to_broadcast([P, IB, P]), iwin[:, :].unsqueeze(1)
                                                .to_broadcast([P, IB, P]), ALU.is_equal).then_inc(pl_hot, 1)
                steps = iwin[:, 0:NSTEP]
                ch.done(nc.vector.memset(eidf, 0.0))
                for e in range(NX - 1):
                    ch.done(nc.vector.tensor_scalar(mask, steps, cumt[:, e:e + 1], None, ALU.is_ge))
                    ch.done(nc.vector.tensor_tensor(eidf, eidf, mask, ALU.add))
                ch.done(nc.vector.tensor_copy(eid_i, eidf[0:1, :]))
                v.wait_ge(inv_ok, 1)
                ch.done(nc.vector.tensor_copy(held, ps[6][:, 0:NTILE]))
                ch.done(nc.vector.tensor_scalar(pad, held, 0.5, None, ALU.is_lt))
                ch.done(nc.vector.tensor_tensor(pad, pad, dump, ALU.mult))
                ch.done(nc.vector.scalar_tensor_tensor(pad, held, -1.0, pad, ALU.add, ALU.add))
                ch.done(nc.vector.tensor_copy(sct, pad))
                ch.done(nc.vector.tensor_scalar(held, held, -1.0, 0.0, ALU.add, ALU.max))
                ch.done(nc.vector.tensor_copy(held_i, held))
                ch.done(nc.vector.tensor_scalar(gat, held_i, 1, None, ALU.arith_shift_right))

        over(phase)

        w1r = RG[:, :].rearrange("p (s f) -> p s f", s=4)
        xr = R2[:, 0:4 * D].rearrange("p (s f) -> p s f", s=4)
        yr = R2[:, 4 * D:8 * D].rearrange("p (s f) -> p s f", s=4)
        ur = R2[:, 8 * D:10 * D].rearrange("p (s k n) -> p s k n", s=2, k=KC)
        hr = R2[:, 10 * D:10 * D + 2 * HID].rearrange("p (s h n) -> p s h n", s=2, h=HC)
        b2s = R2[:, 16 * D:16 * D + NX * D].rearrange("p (e f) -> p e f", e=NX)

        phase = []
        with nc.Block() as block:
            b2_in = semaphore(phase, "e_b2_in")
            x_in = [semaphore(phase, f"e_x{k}") for k in range(4)]
            w_in = [semaphore(phase, f"e_w{k}") for k in range(4)]
            xt_ps = semaphore(phase, "e_xT_psum")
            u_ok = semaphore(phase, "e_xT_ready")
            h_ps = semaphore(phase, "e_h_psum")
            h_ok = semaphore(phase, "e_gelu")
            y_ps = semaphore(phase, "e_y_psum")
            y_ok = semaphore(phase, "e_y_ready")
            y_out = [semaphore(phase, f"e_y_stored{k}") for k in range(4)]
            idx_ok = semaphore(phase, "e_indices")
            turns = semaphore(phase, "e_turns")

            psX, psH, psY = [ps[0], ps[1]], [ps[2], ps[3]], [ps[4], ps[5]]
            LOOPS = (NTILE - 1) // 4

            @block.sync
            def _(sp):
                sp.dma_start(R2[:, 16 * D:16 * D + NX * D], a_b2.unsqueeze(0).to_broadcast([P, NX * D])).then_inc(b2_in, 16)

                def fetch(t, s):
                    e = nc.sync.value_load(eid_i[0:1, bass.ds(t, 1)], min_val=0, max_val=NX - 1)
                    sp.wait_ge(h_ok, t + 1)
                    sp.dma_start(w1r[:, s, :], a_w1[bass.ds(e, 1), :, :].rearrange("a p f -> (a p) f")).then_inc(w_in[s], 16)

                fetch(0, 0)
                fetch(1, 1)
                with nc.sync.Fori(0, LOOPS) as i:
                    for u in range(4):
                        fetch(i * 4 + (u + 2), (u + 2) % 4)
                sp.wait_ge(b2_in, 16)
                for s in range(4):
                    sp.wait_ge(w_in[s], 16 * (LOOPS + (1 if s < 2 else 0)))

            @block.tensor
            def _(pe):
                pe.sem_inc(u_ok, 2)
                pe.sem_inc(y_ps, 2)

                def flip(t, s, turn):
                    pe.wait_ge(x_in[s], turn * 16 + 16)
                    pe.wait_ge(u_ok, t + 1)
                    for k in range(KC):
                        last = nc.tensor.transpose(psX[s % 2][:, k * P:(k + 1) * P], xr[:, s, k * P:(k + 1) * P],
                                                   ident[:, :])
                    last.then_inc(xt_ps, 1)

                def hidden(t, s, turn):
                    pe.wait_ge(w_in[s], turn * 16 + 16)
                    pe.wait_ge(u_ok, t + 3)
                    pe.wait_ge(h_ok, t + 3)
                    for h in range(HC):
                        for k in range(KC):
                            last = nc.tensor.matmul(psH[s % 2][:, h * P:(h + 1) * P],
                                                    w1r[:, s, k * HID + h * P:k * HID + (h + 1) * P],
                                                    ur[:, s % 2, k, :], start=k == 0, stop=k == KC - 1)
                    last.then_inc(h_ps, 1)

                def rows(t, s):
                    e = nc.tensor.value_load(eid_i[0:1, bass.ds(t, 1)], min_val=0, max_val=NX - 1)
                    pe.wait_ge(h_ok, t + 5)
                    pe.wait_ge(y_ok, t + 1)
                    for h in range(HC):
                        last = nc.tensor.matmul(psY[s % 2][:, 0:D], hr[:, s % 2, h, :],
                                                w2_sb[:, bass.ds(e, 1), h, :].rearrange("p a f -> p (a f)"),
                                                start=h == 0, stop=h == HC - 1)
                    last.then_inc(y_ps, 1)

                flip(0, 0, 0)
                flip(1, 1, 0)
                hidden(0, 0, 0)
                with nc.tensor.Fori(0, LOOPS) as i:
                    for u in range(4):
                        flip(i * 4 + (u + 2), (u + 2) % 4, i + (u + 2) // 4)
                        hidden(i * 4 + (u + 1), (u + 1) % 4, i + (u + 1) // 4)
                        rows(i * 4 + u, u)
                rows(NTILE - 1, 0)

            @block.scalar
            def _(act):
                act.sem_inc(h_ok, 4)

                def gelu(t, s):
                    act.wait_ge(h_ps, t + 1)
                    act.wait_ge(y_ps, t + 1)
                    for h in range(HC):
                        last = act.activation(hr[:, s % 2, h, :], psH[s % 2][:, h * P:(h + 1) * P], ACT.Gelu,
                                              bias=w1r[:, s, KC * HID + h:KC * HID + h + 1])
                    last.then_inc(h_ok, 1)

                gelu(0, 0)
                with nc.scalar.Fori(0, LOOPS) as i:
                    for u in range(4):
                        gelu(i * 4 + (u + 1), (u + 1) % 4)

            @block.vector
            def _(v):
                v.sem_inc(y_ok, 2)

                def widen(t, s):
                    v.wait_ge(xt_ps, t + 1)
                    for k in range(KC):
                        last = nc.vector.tensor_scalar(ur[:, s % 2, k, :], psX[s % 2][:, k * P:(k + 1) * P],
                                                       gamma[:, k:k + 1], beta[:, k:k + 1], ALU.mult, ALU.add)
                    last.then_inc(u_ok, 1)

                def bias(t, s, turn):
                    e = nc.vector.value_load(eid_i[0:1, bass.ds(t, 1)], min_val=0, max_val=NX - 1)
                    v.wait_ge(y_ps, t + 3)
                    if not (isinstance(turn, int) and turn == 0):
                        v.wait_ge(y_out[s], turn * 16)
                    nc.vector.tensor_tensor(yr[:, s, :], psY[s % 2][:, 0:D],
                                            b2s[:, bass.ds(e, 1), :].rearrange("p a f -> p (a f)"),
                                            ALU.add).then_inc(y_ok, 1)

                widen(0, 0)
                widen(1, 1)
                v.wait_ge(b2_in, 16)
                for t in range(4):
                    widen(t + 2, (t + 2) % 4)
                    bias(t, t, 0)
                with nc.vector.Fori(1, LOOPS) as i:
                    for u in range(4):
                        widen(i * 4 + (u + 2), (u + 2) % 4)
                        bias(i * 4 + u, u, i)
                bias(NTILE - 1, 0, LOOPS)

            @block.gpsimd
            def _(pool):
                def gather(t, s):
                    pool.wait_ge(u_ok, t - 1)
                    nc.gpsimd.tensor_copy(idxb[:, 0, s:s + 1], gat[:, bass.ds(t, 1)]).then_inc(idx_ok, 1)
                    pool.wait_ge(idx_ok, t * 2 - 6)
                    pool.sem_inc(turns, 1)
                    rows_in(s)

                def rows_in(s):
                    nc.gpsimd.indirect_dma_start(
                        out=xr[:, s, :], out_offset=None, in_=table,
                        in_offset=bass.IndirectOffsetOnAxis(ap=idxb[:, 0, s:s + 1], axis=0)).then_inc(x_in[s], 16)

                def scatter(t, s, behind=0):
                    pool.wait_ge(y_ok, t + 3)
                    nc.gpsimd.tensor_copy(idxb[:, 1, s:s + 1], sct[:, bass.ds(t, 1)]).then_inc(idx_ok, 1)
                    pool.wait_ge(idx_ok, t * 2 + (3 - behind))
                    pool.sem_inc(turns, 1)
                    nc.gpsimd.indirect_dma_start(
                        out=results, out_offset=bass.IndirectOffsetOnAxis(ap=idxb[:, 1, s:s + 1], axis=0),
                        in_=yr[:, s, :], in_offset=None).then_inc(y_out[s], 16)

                nc.gpsimd.tensor_copy(idxb[:, 0, 0:4], gat[:, 0:4]).then_inc(idx_ok, 1)
                pool.wait_ge(idx_ok, 1)
                for s in range(4):
                    rows_in(s)
                with nc.gpsimd.Fori(0, LOOPS - 1) as i:
                    for u in range(4):
                        gather(i * 4 + (u + 4), u)
                        scatter(i * 4 + u, u)
                gather(NTILE - 1, 0)
                pool.wait_ge(u_ok, NTILE - 1)
                rows_in(1)
                for n in range(5):
                    scatter(NTILE - 5 + n, n % 4, n)
                for s in range(4):
                    pool.wait_ge(y_out[s], 16 * (LOOPS + (1 if s == 0 else 0)))

        over(phase)

        RS = 8
        pairs = RG[:, 0:RS * 2 * D].rearrange("p (s f) -> p s f", s=RS)
        assert T % RS == 1

        phase = []
        with nc.Block() as block:
            got = [semaphore(phase, f"o_rows{k}") for k in range(RS)]
            mid = semaphore(phase, "o_first_added")
            ok = semaphore(phase, "o_ready")
            stored = [semaphore(phase, f"o_stored{k}") for k in range(RS)]

            @block.sync
            def _(sp):
                def load(t, s, n=P):
                    sp.dma_start(pairs[0:n, s, :], results[bass.ds(t * (2 * P), 2 * n), :]
                                 .rearrange("(p k) f -> p (k f)", k=2)).then_inc(got[s], 16)

                for s in range(RS):
                    load(s, s)
                with nc.sync.Fori(1, T // RS) as i:
                    for s in range(RS):
                        sp.wait_ge(stored[s], i * 16)
                        load(i * RS + s, s)
                sp.wait_ge(stored[0], T // RS * 16)
                load(T - 1, 0, TAIL)

            @block.vector
            def _(v):
                def combine(t, s, turn, n=P):
                    v.wait_ge(got[s], turn * 16 + 16)
                    x1 = o_all[0:n, bass.ds(t, 1), :].rearrange("p a f -> p (a f)")
                    nc.vector.scalar_tensor_tensor(slotb[0:n, s % 2, :], pairs[0:n, s, 0:D], w1c[0:n, bass.ds(t, 1)],
                                                   x1, ALU.mult, ALU.add).then_inc(mid, 1)
                    v.wait_ge(mid, t + 1)
                    nc.vector.scalar_tensor_tensor(pairs[0:n, s, 0:D], pairs[0:n, s, D:2 * D],
                                                   w2c[0:n, bass.ds(t, 1)], slotb[0:n, s % 2, :], ALU.mult,
                                                   ALU.add).then_inc(ok, 1)

                with nc.vector.Fori(0, T // RS) as i:
                    for s in range(RS):
                        combine(i * RS + s, s, i)
                combine(T - 1, 0, T // RS, TAIL)

            @block.scalar
            def _(act):
                with nc.scalar.Fori(0, T // RS) as i:
                    for s in range(RS):
                        act.wait_ge(ok, i * RS + (s + 1))
                        act.dma_start(a_out[bass.ds((i * RS + s) * P, P), :], pairs[:, s, 0:D]).then_inc(stored[s], 16)
                act.wait_ge(ok, T)
                act.dma_start(a_out[(T - 1) * P:N, :], pairs[0:TAIL, 0, 0:D]).then_inc(stored[0], 16)
                for s in range(RS):
                    act.wait_ge(stored[s], 16 * (T // RS + (1 if s == 0 else 0)))


def kernel(x, src, dst, L0_gnn_W, L0_gnn_conv_bias, L0_gnn_ln_weight, L0_gnn_ln_bias, L0_gnn_prelu_a, L0_mix_t,
           L0_mix_w_qkv, L0_mix_mem_kv, L0_mix_w_out, L0_mix_b_out, L0_mix_g_out, L0_mix_g_pre, L0_ffn_gamma,
           L0_ffn_beta, L0_ffn_Wr, L0_ffn_br, L0_ffn_W1, L0_ffn_b1, L0_ffn_W2, L0_ffn_b2):
    import numpy as np
    import concourse.bacc as bacc
    from concourse.bass_utils import run_bass_kernel_spmd

    def halves(a):
        return np.asarray(a).reshape(KC, P).T.reshape(-1)

    memory = np.asarray(L0_mix_mem_kv).reshape(2, HEADS * DH, MEM)
    w1 = np.asarray(L0_ffn_W1).reshape(NX, KC, P, HID).transpose(0, 2, 1, 3).reshape(NX, P, KC * HID)
    b1 = np.asarray(L0_ffn_b1).reshape(NX, HC, P).transpose(0, 2, 1)
    w2 = np.asarray(L0_ffn_W2).reshape(NX, HC, P, D).transpose(2, 0, 1, 3).reshape(P, NX * HC * D)
    ins = {
        "x": x, "src": src, "dst": dst, "gw": L0_gnn_W, "cb": L0_gnn_conv_bias, "lnw": L0_gnn_ln_weight,
        "lnb": L0_gnn_ln_bias, "pre": L0_gnn_prelu_a, "wqkv": L0_mix_w_qkv, "mk": memory[0], "mv": memory[1],
        "wout": L0_mix_w_out, "bout": L0_mix_b_out, "gout": L0_mix_g_out, "gpre": halves(L0_mix_g_pre),
        "gamma": halves(L0_ffn_gamma), "beta": halves(L0_ffn_beta), "wr": L0_ffn_Wr, "br": L0_ffn_br,
        "w1": np.concatenate([w1, b1], axis=2), "w2": w2, "b2": np.asarray(L0_ffn_b2).reshape(-1),
    }
    nc = bacc.Bacc("TRN2", target_bir_lowering=False, num_devices=1)
    arrays, args = {}, []
    for name, a in ins.items():
        a = np.ascontiguousarray(a)
        arrays[f"in_{name}"] = a
        args.append(nc.dram_tensor(f"in_{name}", a.shape, mybir.dt.from_np(a.dtype), kind="ExternalInput").ap())
    out = nc.dram_tensor("out", (N, D), f32, kind="ExternalOutput").ap()
    build(nc, *args, out)
    r = run_bass_kernel_spmd(nc, [arrays], core_ids=[0])
    return r.results[0]["out"]
```

```python
import concourse.bass as bass
from concourse import mybir
from contextlib import ExitStack

f32, i32, bf16 = mybir.dt.float32, mybir.dt.int32, mybir.dt.bfloat16
ALU, ACT, AX = mybir.AluOpType, mybir.ActivationFunctionType, mybir.AxisListType
P = 128

N, E, D = 6250, 100000, 256
NX, HID, EPS = 8, 512, 1e-5
HEADS, DH, MEM = 4, 32, 4
KC = D // P
HC = HID // P
T = -(-N // P)
TAIL = N - (T - 1) * P
NP = T * P
GC = 4
GE = GC * P
NG = -(-E // GE)
GH = NG // 2
WIN = 96
NC = NG * GC
OHC = 14
OHB = NC // OHC
ACCW = (N // WIN + 1) * WIN + 16
assert ACCW >= N + WIN and NG == 2 * GH and NG == 4 * T and NC % (2 * OHC) == 0 and T % 4 == 1
PADNODE = 8191
SW = -(-N // WIN)
NTILE = (2 * N + NX * (P - 1)) // P
NSTEP = NTILE + 1
assert (NTILE - 1) % 4 == 0
IB = 7
NB = 7
assert 2 * T == 2 * NB * IB
ZS = 16
UN = 4
U = T // UN
KVW = 2 * HEADS * DH + 1
W1ROW = KC * HID + HC


def build(nc, a_x, a_src, a_dst, a_gw, a_cb, a_lnw, a_lnb, a_pre, a_wqkv, a_mk, a_mv, a_wout, a_bout,
          a_gout, a_gpre, a_gamma, a_beta, a_wr, a_br, a_w1, a_w2, a_b2, a_out):
    table = nc.dram_tensor("table", (N, D), f32, kind="Internal").ap()
    results = nc.dram_tensor("results", (2 * N + NTILE * P, D), f32, kind="Internal").ap()
    with ExitStack() as ctx:
        def sb(name, shape, dt=f32):
            return ctx.enter_context(nc.sbuf_tensor(name, shape, dt))

        def semaphore(phase, name):
            phase.append(nc.alloc_semaphore(name))
            return phase[-1]

        def over(phase):
            nc.clear_and_free_semaphores(phase)
            nc.all_engine_barrier()

        R1 = sb("R1", [P, T * KVW])
        R2 = sb("R2", [P, KC * NP])
        R3 = sb("R3", [P, KC * ACCW])
        RG = sb("RG", [P, 4 * W1ROW])
        x_all = R1[:, 0:T * D].rearrange("p (t f) -> p t f", f=D)
        kv = R1[:, :].rearrange("p (t f) -> p t f", f=KVW)
        o_all = x_all
        zT = R2[:, :].rearrange("p (k n) -> p k n", k=KC)
        y_all = R2[:, :].rearrange("p (t f) -> p t f", f=D)
        acc = R3[:, :].rearrange("p (k n) -> p k n", k=KC)
        grows = RG[:, 0:16 * D].rearrange("p (s f) -> p s f", f=D)

        dstrel = sb("dstrel", [P, NG + 1, GC])
        dslow = sb("dslow", [P, NG, GC])
        srci = sb("srci", [P, NG, GC], i32)
        idxb = sb("idxb", [P, 2, 16], i32)
        base_i = sb("base_i", [1, NG], i32)
        flag_i = sb("flag_i", [1, 1], i32)
        ident = sb("ident", [P, P])
        ones = sb("ones", [P, P])
        tri = sb("tri", [P, P])
        bmask = sb("bmask", [P, P])
        iwin = sb("iwin", [P, P])
        valid = sb("valid", [P, 1])
        negbig = sb("negbig", [P, 1])
        wqkv = sb("wqkv", [P, KC, 384])
        gw = sb("gw", [P, KC, D])
        gpre = sb("gpre", [P, KC])
        gamma = sb("gamma", [P, KC])
        beta = sb("beta", [P, KC])
        wr = sb("wr", [P, KC, NX])
        wout = sb("wout", [P, D])
        cw = sb("cw", [P, D])
        bout = sb("bout", [P, D])
        gout = sb("gout", [P, D])
        cbias = sb("cbias", [P, D])
        lnw = sb("lnw", [P, D])
        lnb = sb("lnb", [P, D])
        pre = sb("pre", [P, 1])
        brr = sb("brr", [P, NX])
        mk = sb("mk", [P, MEM])
        mvv = sb("mvv", [P, MEM])
        stats = sb("stats", [P, T, 6])
        mv = sb("mv", [P, T, 2])
        deg = sb("deg", [P, T])
        dinv = sb("dinv", [P, T])
        rstd = sb("rstd", [P, T])
        zs_s = sb("zs_s", [P, T])
        zs_b = sb("zs_b", [P, T])
        cq = sb("cq", [P, T])
        x1s = sb("x1s", [P, T])
        x1b = sb("x1b", [P, T])
        ssq = sb("ssq", [P, T])
        sa = sb("sa", [P, T])
        sc = sb("sc", [P, T])
        sd = sb("sd", [P, T])
        slot = sb("slot", [P, 4, D])
        slotb = sb("slotb", [P, 2, D])
        ksl = sb("ksl", [P, 2, P])
        esl = sb("esl", [P, 2, 132])
        qsl = sb("qsl", [P, 2, P])
        qtl = sb("qtl", [P, 2, P])
        small = sb("small", [P, 64])
        S_t = sb("S_t", [P, 2, GC, WIN])

        ps = [ctx.enter_context(nc.psum_tensor(f"ps{i}", [P, 512], f32)) for i in range(8)]

        def window(k):
            return ps[k][:, 0:KC * WIN].rearrange("p (h w) -> p h w", h=KC)

        class Chain:

            def __init__(self, eng, s, start=0):
                self.eng, self.s, self.n = eng, s, start

            def done(self, ins):
                self.n = self.n + 1
                ins.then_inc(self.s, 1)
                self.eng.wait_ge(self.s, self.n)

        dst_ld = R3[:, 0:1024].bitcast(i32).rearrange("p (h e) -> p h e", h=2)
        src_ld = R3[:, 1024:2048].bitcast(i32).rearrange("p (h e) -> p h e", h=2)
        dstf = R3[:, 2048:3072].rearrange("p (h e) -> p h e", h=2)
        relf = R3[:, 3072:4096].rearrange("p (h e) -> p h e", h=2)
        srcf = R3[:, 4096:5120].rearrange("p (h e) -> p h e", h=2)
        tmpf = R3[:, 5120:6144].rearrange("p (h e) -> p h e", h=2)
        dT = R3[:, 6144:6144 + NC].rearrange("p (g c) -> p g c", c=GC)
        dTi = R3[:, 7000:7000 + NC].bitcast(i32)
        hiI = R3[:, 7800:7800 + NC].bitcast(i32)
        loI = R3[:, 8600:8600 + NC].bitcast(i32)
        hiB = R3[:, 9400:9400 + NC // 2].bitcast(bf16)
        loB = R3[:, 9800:9800 + NC // 2].bitcast(bf16)
        iox = RG[:, 0:P * OHC // 2].bitcast(bf16).rearrange("p (j c) -> p j c", c=OHC)
        ohlo = [RG[:, 1000 + 1300 * k:1000 + 1300 * k + P * OHC // 2].bitcast(bf16)
                .rearrange("p (j c) -> p j c", c=OHC) for k in range(2)]
        ohhi = [RG[:, 1900 + 1300 * k:1900 + 1300 * k + T * OHC // 2].bitcast(bf16)
                .rearrange("p (j c) -> p j c", c=OHC) for k in range(2)]
        zeroB = slotb[:, 0, 0:P // 2].bitcast(bf16)
        zslot = RG[:, 0:ZS * D].rearrange("p (s f) -> p s f", s=ZS)
        root3, val3, tmp3 = (RG[:, 3560 + 3 * T * k:3560 + 3 * T * (k + 1)] for k in range(3))
        negmean, total_x = sd[:, :], sa[:, :]
        iwin_i = slotb[:, 1, 0:P].bitcast(i32)
        cols = sb("cols", [P, 8])
        FULL = GH * GE
        LASTG = E - (NG - 1) * GE

        phase = []
        with nc.Block() as block:
            pads = semaphore(phase, "p_pads")
            e_in = semaphore(phase, "p_edges_in")
            x_in = [semaphore(phase, f"p_x_in{k}") for k in range(7)]
            w_in = semaphore(phase, "p_weights_in")
            const = semaphore(phase, "p_const")
            dv = semaphore(phase, "p_dve_order")
            pl = semaphore(phase, "p_pool_order")
            rel_ok = semaphore(phase, "p_rel_ready")
            tr_ok = semaphore(phase, "p_transposed")
            tr_ev = semaphore(phase, "p_transposed_copied")
            bt_ok = semaphore(phase, "p_base_transposed")
            oh_ok = semaphore(phase, "p_onehots_ready")
            oh_free = semaphore(phase, "p_onehots_free")
            deg_ok = semaphore(phase, "p_deg_ready")
            root_in = semaphore(phase, "p_root_in")
            root_ok = semaphore(phase, "p_root_done")
            aff_ok = semaphore(phase, "p_affine_ready")
            z_ok = semaphore(phase, "p_z_ready")
            sum_ok = semaphore(phase, "p_sums")
            zt_ps = semaphore(phase, "p_zT_psum")
            zt_ok = semaphore(phase, "p_zT_copied")
            tw = [semaphore(phase, f"p_table{k}") for k in range(4)]

            @block.sync
            def _(sp):
                sp.wait_ge(pads, 2)
                for src_, dst_ in ((a_dst, dst_ld), (a_src, src_ld)):
                    sp.dma_start(dst_[0:GH, 0, :], src_[0:FULL].rearrange("(p e) -> p e", e=GE)).then_inc(e_in, 16)
                    sp.dma_start(dst_[0:GH - 1, 1, :],
                                 src_[FULL:2 * FULL - GE].rearrange("(p e) -> p e", e=GE)).then_inc(e_in, 16)
                    sp.dma_start(dst_[GH - 1:GH, 1, 0:LASTG],
                                 src_[2 * FULL - GE:E].rearrange("(p e) -> p e", p=1)).then_inc(e_in, 16)
                sp.wait_ge(pads, 3)
                for k in range(7):
                    lo, hi = 7 * k, min(7 * k + 7, T - 1)
                    sp.dma_start(x_all[:, lo:hi, :],
                                 a_x[lo * P:hi * P, :].rearrange("(t p) f -> p t f", p=P)).then_inc(x_in[k], 16)
                sp.dma_start(x_all[0:TAIL, T - 1, :], a_x[(T - 1) * P:N, :]).then_inc(x_in[6], 16)
                def write(q, h):
                    sp.wait_ge(z_ok, q * 4 + 4)
                    sp.dma_start(table[bass.ds(q * (4 * P), 4 * P), :].rearrange("(t p) f -> p t f", p=P),
                                 zslot[:, 4 * h:4 * h + 4, :]).then_inc(tw[h], 16)

                with nc.sync.Fori(0, T // ZS) as i:
                    for h in range(4):
                        write(i * 4 + h, h)
                sp.wait_ge(z_ok, T)
                sp.dma_start(table[(T - 1) * P:N, :], zslot[0:TAIL, 0, :]).then_inc(tw[0], 16)
                for h in range(4):
                    sp.wait_ge(tw[h], 16 * (T // ZS + (1 if h == 0 else 0)))

            @block.scalar
            def _(act):
                for d_, s_ in (
                    (wqkv[:, :, :], a_wqkv.rearrange("(k p) n -> p k n", p=P)),
                    (gw[:, :, :], a_gw.rearrange("(k p) n -> p k n", p=P)),
                    (gpre[:, :], a_gpre.rearrange("(p k) -> p k", k=KC)),
                    (gamma[:, :], a_gamma.rearrange("(p k) -> p k", k=KC)),
                    (beta[:, :], a_beta.rearrange("(p k) -> p k", k=KC)),
                    (wr[:, :, :], a_wr.rearrange("(k p) n -> p k n", p=P)),
                    (wout[:, :], a_wout),
                    (bout[:, :], a_bout.unsqueeze(0).to_broadcast([P, D])),
                    (gout[:, :], a_gout.unsqueeze(0).to_broadcast([P, D])),
                    (cbias[:, :], a_cb.unsqueeze(0).to_broadcast([P, D])),
                    (lnw[:, :], a_lnw.unsqueeze(0).to_broadcast([P, D])),
                    (lnb[:, :], a_lnb.unsqueeze(0).to_broadcast([P, D])),
                    (pre[:, :], a_pre.unsqueeze(0).to_broadcast([P, 1])),
                    (brr[:, :], a_br.unsqueeze(0).to_broadcast([P, NX])),
                    (mk[:, :], a_mk), (mvv[:, :], a_mv),
                ):
                    act.dma_start(d_, s_).then_inc(w_in, 16)
                for n, dest in enumerate((dT, dstrel, srci)):
                    for h in range(2):
                        act.wait_ge(tr_ok, 2 * n + h + 1)
                        act.activation(dest[:, h * GH:(h + 1) * GH, :].rearrange("p g c -> p c g"),
                                       ps[2 * n + h][:, 0:GC * GH].rearrange("p (c g) -> p c g", c=GC),
                                       ACT.Copy).then_inc(tr_ev, 1)
                for k in range(7):
                    act.wait_ge(x_in[k], 16 * (2 if k == 6 else 1))

                def sums(t, u):
                    act.activation(slot[:, u, :], x_all[:, bass.ds(t, 1), :].rearrange("p a f -> p (a f)"),
                                   ACT.Copy, accum_out=total_x[:, bass.ds(t, 1)]).then_inc(sum_ok, 1)
                    act.wait_ge(sum_ok, t + 1)

                def squares(t, u):
                    act.activation(slot[:, u, :], x_all[:, bass.ds(t, 1), :].rearrange("p a f -> p (a f)"),
                                   ACT.Square, bias=negmean[:, bass.ds(t, 1)],
                                   accum_out=ssq[:, bass.ds(t, 1)]).then_inc(sum_ok, 1)
                    act.wait_ge(sum_ok, t + (T + 2))

                with nc.scalar.Fori(0, U) as i:
                    for u in range(UN):
                        sums(i * UN + u, u)
                sums(T - 1, 0)
                act.activation(negmean, total_x, ACT.Copy, scale=-1.0 / D).then_inc(sum_ok, 1)
                act.wait_ge(sum_ok, T + 1)
                with nc.scalar.Fori(0, U) as i:
                    for u in range(UN):
                        squares(i * UN + u, u)
                squares(T - 1, 0)
                act.wait_ge(root_in, 1)
                act.activation(root3, val3, ACT.Sqrt).then_inc(root_ok, 1)
                act.wait_ge(aff_ok, 1)

                def z_tiles(q, h, turn):
                    if not (isinstance(turn, int) and turn == 0):
                        act.wait_ge(tw[h], turn * 16)
                        act.wait_ge(zt_ps, q * 4 - 12)
                    for u in range(4):
                        act.activation(zslot[:, 4 * h + u, :],
                                       x_all[:, bass.ds(q * 4 + u, 1), :].rearrange("p a f -> p (a f)"),
                                       ACT.Identity, bias=zs_b[:, bass.ds(q * 4 + u, 1)],
                                       scale=zs_s[:, bass.ds(q * 4 + u, 1)]).then_inc(z_ok, 1)

                for h in range(4):
                    z_tiles(h, h, 0)
                with nc.scalar.Fori(1, T // ZS) as i:
                    for h in range(4):
                        z_tiles(i * 4 + h, h, i)
                act.wait_ge(tw[0], T // ZS * 16)
                act.wait_ge(zt_ps, T - ZS)
                act.activation(zslot[:, 0, :], x_all[:, T - 1, :], ACT.Identity, bias=zs_b[:, T - 1:T],
                               scale=zs_s[:, T - 1:T]).then_inc(z_ok, 1)

            @block.gpsimd
            def _(pool):
                n = 0

                def step(ins):
                    nonlocal n
                    n += 1
                    ins.then_inc(pl, 1)
                    pool.wait_ge(pl, n)

                step(nc.gpsimd.memset(ident[:, :], 0.0))
                step(nc.gpsimd.affine_select(out=ident[:, :], in_=ident[:, :], compare_op=ALU.not_equal, fill=1.0,
                                             base=0, pattern=[[-1, P]], channel_multiplier=1))
                pool.sem_inc(const, 1)
                step(nc.gpsimd.iota(iox[:, :, :], pattern=[[1, P], [0, OHC]], base=0, channel_multiplier=0,
                                    allow_small_or_imprecise_dtypes=True))
                step(nc.gpsimd.iota(iwin_i, pattern=[[1, P]], base=0, channel_multiplier=0))
                step(nc.gpsimd.tensor_copy(iwin[:, :], iwin_i))
                pool.sem_inc(const, 1)
                step(nc.gpsimd.memset(ones[:, :], 1.0))
                step(nc.gpsimd.affine_select(out=tri[:, :], in_=ones[:, :], compare_op=ALU.is_gt, fill=0.0,
                                             base=0, pattern=[[1, P]], channel_multiplier=-1))
                step(nc.gpsimd.affine_select(out=valid[:, :], in_=ones[:, 0:1], compare_op=ALU.is_gt, fill=0.0,
                                             base=TAIL, pattern=[[0, 1]], channel_multiplier=-1))
                step(nc.gpsimd.memset(bmask[:, :], 0.0))
                for h in range(HEADS):
                    step(nc.gpsimd.memset(bmask[h * DH:(h + 1) * DH, h * DH:(h + 1) * DH], 1.0))
                pool.sem_inc(const, 1)
                pool.wait_ge(deg_ok, 1)
                nc.gpsimd.memset(acc[:, :, N:ACCW], 0.0).then_inc(pl, 1)

                def own_rows(t):
                    pool.wait_ge(zt_ok, t + 5)
                    nc.gpsimd.tensor_copy(acc[:, :, bass.ds(t * P, P)], zT[:, :, bass.ds(t * P, P)]).then_inc(pl, 1)

                with nc.gpsimd.Fori(0, U) as i:
                    for u in range(0, UN, 2):
                        own_rows(i * UN + u)
                pool.wait_ge(zt_ok, T + 4)
                nc.gpsimd.tensor_copy(acc[:, :, (T - 1) * P:N], zT[:, :, (T - 1) * P:N]).then_inc(pl, 1)
                pool.wait_ge(pl, n + 2 + U * UN // 2)

            @block.tensor
            def _(pe):
                pe.sem_inc(oh_free, 2)
                pe.sem_inc(zt_ok, 4)
                pe.wait_ge(const, 1)
                for n, arr in enumerate((dstf, relf, srcf)):
                    pe.wait_ge(rel_ok, n + 1)
                    for h in range(2):
                        for c in range(GC):
                            last = nc.tensor.transpose(ps[2 * n + h][:, c * GH:(c + 1) * GH],
                                                       arr[0:GH, h, c * P:(c + 1) * P], ident[0:GH, 0:GH])
                        last.then_inc(tr_ok, 1)
                pe.wait_ge(rel_ok, 4)
                for k in range(4):
                    last = nc.tensor.transpose(ps[6][0:1, k * GH:(k + 1) * GH], cols[0:GH, k:k + 1],
                                               ident[0:GH, 0:GH])
                last.then_inc(bt_ok, 1)
                pe.wait_ge(oh_ok, 1)
                nc.tensor.matmul(ps[7][:, 0:T], zeroB, zeroB[:, 0:T], start=True, stop=False)
                with nc.tensor.Fori(0, OHB // 2) as i:
                    for k in range(2):
                        pe.wait_ge(oh_ok, i * 2 + (k + 2))
                        for c in range(OHC):
                            last = nc.tensor.matmul(ps[7][:, 0:T], ohlo[k][:, :, c], ohhi[k][:, :, c],
                                                    start=False, stop=False)
                        last.then_inc(oh_free, 1)
                nc.tensor.matmul(ps[7][:, 0:T], zeroB, zeroB[:, 0:T], start=False, stop=True).then_inc(deg_ok, 1)

                def flip(t, u):
                    pe.wait_ge(z_ok, t + 1)
                    pe.wait_ge(zt_ok, t + 1)
                    for k in range(KC):
                        last = nc.tensor.transpose(ps[u % 4][:, k * P:(k + 1) * P], zslot[:, u, k * P:(k + 1) * P],
                                                   ident[:, :])
                    last.then_inc(zt_ps, 1)

                with nc.tensor.Fori(0, T // ZS) as i:
                    for u in range(ZS):
                        flip(i * ZS + u, u)
                flip(T - 1, 0)

            @block.vector
            def _(v):
                nc.vector.memset(dst_ld[:, 1, :], PADNODE).then_inc(pads, 1)
                nc.vector.memset(src_ld[:, 1, :], 0).then_inc(pads, 1)
                nc.vector.memset(x_all[:, T - 1, :], 0.0).then_inc(pads, 1)
                nc.vector.memset(dstrel[:, NG, :], -1.0)
                nc.vector.memset(zeroB, 0.0).then_inc(oh_ok, 1)
                ch = Chain(v, dv)
                v.wait_ge(e_in, 16 * 6)
                h = slice(0, GH)
                ch.done(nc.vector.tensor_copy(dstf[h, :, :], dst_ld[h, :, :]))
                v.sem_inc(rel_ok, 1)
                ch.done(nc.vector.tensor_reduce(cols[h, 0:2], dstf[h, :, :], AX.X, ALU.min))
                for k in range(2):
                    ch.done(nc.vector.tensor_scalar(relf[h, k, :], dstf[h, k, :], cols[h, k:k + 1], None,
                                                    ALU.subtract))
                v.sem_inc(rel_ok, 1)
                ch.done(nc.vector.tensor_copy(srcf[h, :, :], src_ld[h, :, :]))
                v.sem_inc(rel_ok, 1)
                ch.done(nc.vector.tensor_scalar(tmpf[h, :, :], dstf[h, :, :], float(N), None, ALU.is_lt))
                ch.done(nc.vector.tensor_tensor(tmpf[h, :, :], tmpf[h, :, :], relf[h, :, :], ALU.mult))
                ch.done(nc.vector.tensor_reduce(cols[h, 2:4], tmpf[h, :, :], AX.X, ALU.max))
                v.sem_inc(rel_ok, 1)
                v.wait_ge(tr_ev, 2)
                dflat = dT.rearrange("p g c -> p (g c)")
                ch.done(nc.vector.tensor_copy(dTi, dflat))
                ch.done(nc.vector.tensor_scalar(hiI, dTi, 7, None, ALU.arith_shift_right))
                ch.done(nc.vector.tensor_scalar(loI, dTi, P - 1, None, ALU.bitwise_and))
                ch.done(nc.vector.tensor_copy(hiB, hiI))
                ch.done(nc.vector.tensor_copy(loB, loI))
                v.wait_ge(tr_ev, 4)
                ch.done(nc.vector.tensor_scalar(dslow[:, :, :], dstrel[:, 0:NG, :], float(WIN), -1e6, ALU.is_lt,
                                                ALU.mult))
                ch.done(nc.vector.tensor_tensor(dslow[:, :, :], dslow[:, :, :], dT, ALU.add))
                v.wait_ge(bt_ok, 1)
                ch.done(nc.vector.tensor_copy(base_i[0:1, :], ps[6][0:1, 0:NG]))
                ch.done(nc.vector.tensor_reduce(small[0:1, 0:1], ps[6][0:1, NG:2 * NG], AX.X, ALU.max))
                ch.done(nc.vector.tensor_scalar(flag_i[0:1, :], small[0:1, 0:1], float(WIN), None, ALU.is_ge))
                v.wait_ge(const, 2)

                order = ch.n
                with nc.vector.Fori(0, OHB // 2) as i:
                    for k in range(2):
                        m = i * 2 + k
                        v.wait_ge(oh_free, m + 1)
                        lo = loB[:, bass.ds(m * OHC, OHC)].unsqueeze(1)
                        hi = hiB[:, bass.ds(m * OHC, OHC)].unsqueeze(1)
                        nc.vector.tensor_tensor(ohlo[k], lo.to_broadcast([P, P, OHC]), iox, ALU.is_equal)
                        nc.vector.tensor_tensor(ohhi[k], hi.to_broadcast([P, T, OHC]), iox[:, 0:T, :],
                                                ALU.is_equal).then_inc(oh_ok, 1)
                def rsqrt3(outs):
                    v.sem_inc(root_in, 1)
                    v.wait_ge(root_ok, 1)
                    ch.done(nc.vector.reciprocal(root3, root3))
                    ch.done(nc.vector.tensor_tensor(tmp3, root3, root3, ALU.mult))
                    ch.done(nc.vector.tensor_tensor(tmp3, tmp3, val3, ALU.mult))
                    ch.done(nc.vector.tensor_scalar(tmp3, tmp3, -0.5, 1.5, ALU.mult, ALU.add))
                    for k, out in enumerate(outs):
                        piece = slice(k * T, (k + 1) * T)
                        ch.done(nc.vector.tensor_tensor(out, root3[:, piece], tmp3[:, piece], ALU.mult))

                ch.n = order
                v.wait_ge(sum_ok, 2 * T + 1)
                var = sc[:, :]
                ch.done(nc.vector.tensor_scalar(var, ssq[:, :], 1.0 / D, None, ALU.mult))
                ch.done(nc.vector.tensor_scalar(val3[:, 0:T], var, EPS, None, ALU.add))
                ch.done(nc.vector.reciprocal(val3[:, T:2 * T], val3[:, 0:T]))
                ch.done(nc.vector.tensor_tensor(val3[:, T:2 * T], val3[:, T:2 * T], var, ALU.mult))
                ch.done(nc.vector.tensor_scalar(val3[:, T:2 * T], val3[:, T:2 * T], float(D), 1e-24, ALU.mult,
                                                ALU.max))
                v.wait_ge(deg_ok, 1)
                ch.done(nc.vector.tensor_scalar(deg[:, :], ps[7][:, 0:T], 1.0, None, ALU.add))
                ch.done(nc.vector.tensor_copy(val3[:, 2 * T:3 * T], deg[:, :]))
                rsqrt3((rstd[:, :], cq[:, :], dinv[:, :]))
                ch.done(nc.vector.tensor_tensor(zs_s[:, :], rstd[:, :], dinv[:, :], ALU.mult))
                ch.done(nc.vector.tensor_tensor(zs_b[:, :], negmean, zs_s[:, :], ALU.mult))
                v.sem_inc(aff_ok, 1)
                ch.done(nc.vector.tensor_tensor(sc[:, :], deg[:, :], dinv[:, :], ALU.mult))
                ch.done(nc.vector.scalar_tensor_tensor(cq[:, :], cq[:, :], float(D) ** 0.5, sc[:, :], ALU.mult,
                                                       ALU.mult))
                ch.done(nc.vector.tensor_scalar(x1s[:, :], rstd[:, :], 1.0, None, ALU.add))
                ch.done(nc.vector.tensor_tensor(x1b[:, :], negmean, rstd[:, :], ALU.mult))
                v.wait_ge(const, 3)
                ch.done(nc.vector.tensor_scalar(negbig[:, :], valid[:, :], 1e30, -1e30, ALU.mult, ALU.add))
                v.wait_ge(w_in, 16 * 16)
                for k in range(KC):
                    ch.done(nc.vector.tensor_scalar(wqkv[:, k, :], wqkv[:, k, :], gpre[:, k:k + 1], None, ALU.mult))

                def keep(t, u):
                    v.wait_ge(zt_ps, t + 1)
                    nc.vector.tensor_copy(zT[:, :, bass.ds(t * P, P)],
                                          ps[u][:, 0:D].rearrange("p (k n) -> p k n", k=KC)).then_inc(zt_ok, 1)

                with nc.vector.Fori(0, U) as i:
                    for u in range(UN):
                        if u % 2 == 1:
                            v.wait_ge(zt_ps, i * UN + (u + 1))
                            nc.vector.tensor_copy(acc[:, :, bass.ds((i * UN + u) * P, P)],
                                                  ps[u][:, 0:D].rearrange("p (k n) -> p k n", k=KC))
                        keep(i * UN + u, u)
                keep(T - 1, 0)

        over(phase)

        TA, TC, TB, TD = (n * T for n in range(4))
        rs = cq
        negM = small[:, 1:2]
        mrow = slotb[:, 0, 0:P]
        emk = small[:, 4:4 + MEM]
        emT = sb("emT", [MEM, P])
        mvT = sb("mvT", [MEM, P + 1])
        cn = slotb[:, 0, P:2 * P]
        cnT = slotb[:, 1, 0:P]
        psA, psC, psT, psO = [ps[2], ps[3]], ps[4], ps[5], [ps[6], ps[7]]

        phase = []
        with nc.Block() as block:
            got = [semaphore(phase, f"a_rows{k}") for k in range(16)]
            idx_ok = semaphore(phase, "a_indices")
            turns = semaphore(phase, "a_turns")
            pe_done = semaphore(phase, "a_group_multiplied")
            s_ok = semaphore(phase, "a_onehots")
            acc_ok = semaphore(phase, "a_group_added")
            zt_ok = semaphore(phase, "a_z_copied")
            mm_ok = semaphore(phase, "a_products")
            kv_ev = semaphore(phase, "a_kv_copied")
            ks_ok = semaphore(phase, "a_keys_less_max")
            ex_ok = semaphore(phase, "a_keys_exp")
            cx_ok = semaphore(phase, "a_context_added")
            m_ok = semaphore(phase, "a_max_ready")
            mem_ok = semaphore(phase, "a_memory_exp")
            mid_pe = semaphore(phase, "a_setup_products")
            mid_dve = semaphore(phase, "a_setup_vector")
            q_ps = semaphore(phase, "a_q_psum")
            q_ev = semaphore(phase, "a_q_copied")
            q_sub = semaphore(phase, "a_q_less_max")
            q_exp = semaphore(phase, "a_q_exp")
            q_n = semaphore(phase, "a_q_normed")
            qt_ps = semaphore(phase, "a_qT_psum")
            qt_ok = semaphore(phase, "a_qT_copied")
            o_ps = semaphore(phase, "a_o_psum")
            o_ok = semaphore(phase, "a_o_ready")
            sq_ok = semaphore(phase, "a_o_squared")
            xs_in = [semaphore(phase, f"a_x{k}") for k in range(UN)]
            xb_ok = semaphore(phase, "a_x_plus_norm")
            on_ok = semaphore(phase, "a_attention_normed")
            res_ok = semaphore(phase, "a_residual_summed")
            root_in = semaphore(phase, "a_root_in")
            root_ok = semaphore(phase, "a_root_done")
            dv = semaphore(phase, "a_dve_order")

            @block.sync
            def _(sp):
                def x_tile(t, u, rows=P):
                    sp.wait_ge(res_ok, t + 1)
                    src_ = a_x[bass.ds(t * P, P), :] if rows == P else a_x[(T - 1) * P:N, :]
                    sp.dma_start(slot[0:rows, u, :], src_).then_inc(xs_in[u], 16)

                sp.wait_ge(q_ps, T)
                with nc.sync.Fori(0, U) as i:
                    for u in range(UN):
                        x_tile(i * UN + u, u)
                x_tile(T - 1, 0, TAIL)

            @block.gpsimd
            def _(pool):
                flat = srci[:, 0:NG, :].rearrange("p g c -> p (g c)")

                def turn(first, half, count):
                    pool.wait_ge(pe_done, first + 1)
                    nc.gpsimd.tensor_copy(idxb[:, half, :], flat[:, bass.ds(first * 4, 16)]).then_inc(idx_ok, 1)
                    pool.wait_ge(idx_ok, count)
                    pool.sem_inc(turns, 1)
                    for s in range(16):
                        if s % 4 == 0 and s:
                            pool.wait_ge(pe_done, first + (s // 4 + 1))
                            pool.sem_inc(turns, 1)
                        nc.gpsimd.indirect_dma_start(
                            out=grows[:, s, :], out_offset=None, in_=table,
                            in_offset=bass.IndirectOffsetOnAxis(ap=idxb[:, half, s:s + 1], axis=0),
                        ).then_inc(got[s], 16)

                with nc.gpsimd.Fori(0, NG // 8) as i:
                    for half in range(2):
                        turn(i * 8 + 4 * half, half, i * 2 + (half + 1))
                turn(NG - 4, 0, NG // 4)

            @block.tensor
            def _(pe):
                pe.sem_inc(pe_done, 4)

                def aggregate(g, r, turn):
                    pe.wait_ge(s_ok, g + 1)
                    pe.wait_ge(acc_ok, g + 1)
                    for h in range(KC):
                        for c in range(GC):
                            if h == 0:
                                pe.wait_ge(got[4 * r + c], turn * 16 + 16)
                            last = nc.tensor.matmul(window(r % 2)[:, h, :], grows[:, 4 * r + c, h * P:(h + 1) * P],
                                                    S_t[:, r % 2, c, :], start=c == 0, stop=c == GC - 1)
                    last.then_inc(pe_done, 1)

                def group(i, base, off):
                    per, g0 = base
                    g = i * (4 * per) + (g0 + off)
                    return g, (g0 + off) % 4, i * per + (g0 + off) // 4

                def keys_values(t, u):
                    pe.wait_ge(zt_ok, t + 1)
                    pe.wait_ge(kv_ev, t + 1)
                    for k in range(KC):
                        last = nc.tensor.matmul(psA[u][:, 0:D], slot[:, u, k * P:(k + 1) * P], wqkv[:, k, P:3 * P],
                                                start=k == 0, stop=k == KC - 1)
                    last.then_inc(mm_ok, 1)

                aggregate(*group(0, (1, TA), 0))
                keys_values(0, 0)
                with nc.tensor.Fori(0, U) as i:
                    for u in range(UN):
                        aggregate(*group(i, (1, TA), 1 + u))
                        keys_values(i * UN + (u + 1), (u + 1) % 2)

                pe.wait_ge(ks_ok, 1)
                nc.tensor.transpose(psT[:, 0:P], cn, ident[:, :]).then_inc(mid_pe, 1)
                pe.wait_ge(mid_dve, 1)
                last = nc.tensor.matmul(psO[0][:, 0:P], ones[:, :], cn, start=True, stop=True)
                last.then_inc(mid_pe, 1)
                pe.wait_ge(mem_ok, 1)
                nc.tensor.transpose(psO[1][0:MEM, 0:P], emk, ident[:, :])
                nc.tensor.transpose(psO[1][0:MEM, P:2 * P], mvv[:, :], ident[:, :]).then_inc(mid_pe, 1)
                pe.wait_ge(mid_dve, 2)
                nc.tensor.matmul(psC[:, 0:P + 1], emT[:, :], mvT[:, :], start=True, stop=False,
                                 skip_group_check=True)

                def context(t, u):
                    pe.wait_ge(ex_ok, t + 3)
                    nc.tensor.matmul(psC[:, 0:P + 1], esl[:, u, 0:P],
                                     kv[:, bass.ds(t, 1), P:2 * P + 1].rearrange("p a f -> p (a f)"),
                                     start=False, stop=False, skip_group_check=True).then_inc(cx_ok, 1)

                aggregate(*group(0, (1, TC), 0))
                context(0, 0)
                with nc.tensor.Fori(0, U) as i:
                    for u in range(UN):
                        aggregate(*group(i, (1, TC), 1 + u))
                        context(i * UN + (u + 1), (u + 1) % 2)

                pe.wait_ge(mid_dve, 3)
                nc.tensor.transpose(psT[:, 0:P], cn, ident[:, :]).then_inc(mid_pe, 1)
                pe.wait_ge(mid_dve, 4)
                nc.tensor.matmul(psO[0][:, 0:D], cnT, wout[:, :], start=True, stop=True).then_inc(mid_pe, 1)

                def queries(t, u):
                    pe.wait_ge(zt_ok, t + (T + 1))
                    for k in range(KC):
                        last = nc.tensor.matmul(psA[u][:, 0:P], slot[:, u, k * P:(k + 1) * P], wqkv[:, k, 0:P],
                                                start=k == 0, stop=k == KC - 1)
                    last.then_inc(q_ps, 1)

                def flip(t, u):
                    pe.wait_ge(q_n, t + 1)
                    nc.tensor.transpose(psT[:, 0:P], ksl[:, u, :], ident[:, :]).then_inc(qt_ps, 1)

                def attend(t, u):
                    pe.wait_ge(qt_ok, t + 1)
                    pe.wait_ge(o_ok, t + 1)
                    nc.tensor.matmul(psO[u][:, 0:D], qtl[:, u, :], cw[:, :], start=True, stop=True).then_inc(o_ps, 1)

                def step(i, j, g):
                    t = j if i is None else i * UN + j
                    if g < T - 1:
                        queries(t + 1, (j + 1) % 2)
                    if g < T:
                        aggregate(*group(0 if i is None else i, (1, TB), j))
                        flip(t, j % 2)
                    if g > 0:
                        attend(t - 1, (j - 1) % 2)

                queries(0, 0)
                step(None, 0, 0)
                pe.wait_ge(mid_dve, 5)
                for j in range(1, UN):
                    step(None, j, j)
                with nc.tensor.Fori(1, U) as i:
                    for u in range(UN):
                        step(i, u, UN)
                for j in range(T - 1, T + 1):
                    step(None, j, j)
                with nc.tensor.Fori(0, U) as i:
                    for u in range(UN):
                        aggregate(*group(i, (1, TD), u))
                aggregate(*group(0, (1, TD), T - 1))

            @block.scalar
            def _(act):
                act.sem_inc(kv_ev, 2)
                act.sem_inc(cx_ok, 2)

                def z_copy(t, u):
                    act.activation(slot[:, u, :].rearrange("p (k n) -> p k n", k=KC), zT[:, :, bass.ds(t * P, P)],
                                   ACT.Copy).then_inc(zt_ok, 1)

                def kv_out(t, u):
                    act.wait_ge(mm_ok, t + 1)
                    act.activation(kv[:, bass.ds(t, 1), 0:2 * P].rearrange("p a f -> p (a f)"), psA[u][:, 0:D],
                                   ACT.Copy, scale=cq[:, bass.ds(t, 1)]).then_inc(kv_ev, 1)

                z_copy(0, 0)
                with nc.scalar.Fori(0, U) as i:
                    for u in range(UN):
                        z_copy(i * UN + (u + 1), (u + 1) % 2)
                        kv_out(i * UN + u, u % 2)
                kv_out(T - 1, 0)

                act.wait_ge(m_ok, 1)
                act.activation(emk, mk[:, :], ACT.Exp, bias=negM).then_inc(mem_ok, 1)

                def keys_exp(t, u):
                    act.wait_ge(ks_ok, t + 2)
                    act.wait_ge(cx_ok, t + 1)
                    act.activation(esl[:, u, 0:P], ksl[:, u, :], ACT.Exp).then_inc(ex_ok, 1)

                keys_exp(0, 0)
                with nc.scalar.Fori(0, U) as i:
                    for u in range(UN):
                        keys_exp(i * UN + (u + 1), (u + 1) % 2)

                def q_out(t, u):
                    act.wait_ge(q_ps, t + 1)
                    act.activation(qsl[:, u, :], psA[u][:, 0:P], ACT.Copy,
                                   scale=cq[:, bass.ds(t, 1)]).then_inc(q_ev, 1)

                def q_power(t, u):
                    act.wait_ge(q_sub, t + 1)
                    act.activation(qsl[:, u, :], qsl[:, u, :], ACT.Exp).then_inc(q_exp, 1)

                def qt_out(t, u):
                    act.wait_ge(qt_ps, t + 1)
                    act.activation(qtl[:, u, :], psT[:, 0:P], ACT.Copy).then_inc(qt_ok, 1)

                def square(t, u):
                    act.wait_ge(o_ok, t + 3)
                    act.activation(slotb[:, u, :], o_all[:, bass.ds(t, 1), :].rearrange("p a f -> p (a f)"),
                                   ACT.Square, accum_out=ssq[:, bass.ds(t, 1)]).then_inc(sq_ok, 1)
                    act.wait_ge(sq_ok, t + 1)

                def step(i, j, g):
                    t = j if i is None else i * UN + j
                    if 0 < g <= T:
                        qt_out(t - 1, (j - 1) % 2)
                    if g < T - 2:
                        z_copy(t + 2, j % 2)
                    if g < T:
                        q_power(t, j % 2)
                    if g < T - 1:
                        q_out(t + 1, (j + 1) % 2)
                    if g > 2:
                        square(t - 3, (j - 3) % 2)

                z_copy(0, 0)
                z_copy(1, 1)
                q_out(0, 0)
                for j in range(UN):
                    step(None, j, j)
                with nc.scalar.Fori(1, U - 1) as i:
                    for u in range(UN):
                        step(i, u, UN)
                for j in range(T - 1 - UN, T + 3):
                    step(None, j, j)
                act.wait_ge(root_in, 1)
                act.activation(sa[:, :], sc[:, :], ACT.Sqrt).then_inc(root_ok, 1)

                def x_plus_norm(t, u, turn):
                    act.wait_ge(xs_in[u], turn * 16 + 16)
                    act.activation(slot[:, u, :], slot[:, u, :], ACT.Identity, scale=x1s[:, bass.ds(t, 1)],
                                   bias=x1b[:, bass.ds(t, 1)]).then_inc(xb_ok, 1)

                with nc.scalar.Fori(0, U) as i:
                    for u in range(UN):
                        x_plus_norm(i * UN + u, u, i)
                x_plus_norm(T - 1, 0, U)

            @block.vector
            def _(v):
                v.sem_inc(acc_ok, 2)
                v.sem_inc(ex_ok, 2)
                v.sem_inc(o_ok, 2)
                nc.vector.memset(kv[:, :, 2 * P:2 * P + 1], 1.0)
                nc.vector.memset(mvT[:, P:P + 1], 1.0)

                def onehots(g, r):
                    v.wait_ge(pe_done, g + 3)
                    nc.vector.tensor_tensor(
                        S_t[:, r % 2, :, :],
                        dstrel[:, bass.ds(g, 1), :].rearrange("p g c -> p (g c)").unsqueeze(2).to_broadcast([P, GC, WIN]),
                        iwin[:, 0:WIN].unsqueeze(1).to_broadcast([P, GC, WIN]), ALU.is_equal).then_inc(s_ok, 1)

                def add(g, r):
                    at = nc.vector.value_load(base_i[0:1, bass.ds(g, 1)], min_val=0, max_val=N)
                    v.wait_ge(pe_done, g + 5)
                    v.wait_ge(acc_ok, g + 2)
                    win = acc[:, :, bass.ds(at, WIN)]
                    nc.vector.tensor_tensor(win, win, window(r % 2), ALU.add).then_inc(acc_ok, 1)

                def group(i, base, off):
                    per, g0 = base
                    return i * (4 * per) + (g0 + off), (g0 + off) % 4

                def pair(i, base, off, between=None):
                    g, r = group(i, base, off)
                    onehots(g + 1, r + 1)
                    if between:
                        between()
                    add(g, r)

                onehots(0, 0)
                pair(0, (1, TA), 0)
                with nc.vector.Fori(0, U) as i:
                    for u in range(UN):
                        pair(i, (1, TA), 1 + u)

                ch = Chain(v, dv)
                v.wait_ge(kv_ev, T + 2)
                last = kv[:, T - 1, 0:P]
                ch.done(nc.vector.tensor_scalar(last, last, valid[:, :], negbig[:, :], ALU.mult, ALU.add))
                ch.done(nc.vector.tensor_reduce(cn, kv[:, :, 0:P].rearrange("p t c -> p c t"), AX.X, ALU.max))
                v.sem_inc(ks_ok, 1)
                v.wait_ge(mid_pe, 1)
                ch.done(nc.vector.tensor_reduce(small[:, 0:1], psT[:, 0:P], AX.X, ALU.max))
                ch.done(nc.vector.tensor_reduce(small[:, 2:3], mk[:, :], AX.X, ALU.max))
                ch.done(nc.vector.tensor_tensor(small[:, 0:1], small[:, 0:1], small[:, 2:3], ALU.max))
                ch.done(nc.vector.tensor_scalar(negM, small[:, 0:1], -1.0, None, ALU.mult))
                v.sem_inc(m_ok, 1)
                ch.done(nc.vector.tensor_scalar(cn, ident[:, :], small[:, 0:1], None, ALU.mult))
                v.sem_inc(mid_dve, 1)
                v.wait_ge(mid_pe, 2)
                ch.done(nc.vector.tensor_copy(mrow, psO[0][:, 0:P]))
                v.wait_ge(mid_pe, 3)
                ch.done(nc.vector.tensor_copy(emT[:, :], psO[1][0:MEM, 0:P]))
                ch.done(nc.vector.tensor_copy(mvT[:, 0:P], psO[1][0:MEM, P:2 * P]))
                v.sem_inc(mid_dve, 1)

                def keys_less_max(t, u):
                    v.wait_ge(ex_ok, t + 1)
                    nc.vector.tensor_tensor(ksl[:, u, :], kv[:, bass.ds(t, 1), 0:P].rearrange("p a f -> p (a f)"),
                                            mrow, ALU.subtract).then_inc(ks_ok, 1)

                pair(0, (1, TC), 0, lambda: keys_less_max(0, 0))
                with nc.vector.Fori(0, U) as i:
                    for u in range(UN):
                        pair(i, (1, TC), 1 + u, lambda: keys_less_max(i * UN + (u + 1), (u + 1) % 2))

                v.wait_ge(cx_ok, T + 2)
                ch.done(nc.vector.reciprocal(small[:, 3:4], psC[:, P:P + 1]))
                ch.done(nc.vector.tensor_scalar(cn, psC[:, 0:P], small[:, 3:4], float(DH) ** -0.5, ALU.mult,
                                                ALU.mult))
                ch.done(nc.vector.tensor_tensor(cn, cn, bmask[:, :], ALU.mult))
                v.sem_inc(mid_dve, 1)
                v.wait_ge(mid_pe, 4)
                ch.done(nc.vector.tensor_copy(cnT, psT[:, 0:P]))
                v.sem_inc(mid_dve, 1)
                v.wait_ge(mid_pe, 5)
                ch.done(nc.vector.tensor_copy(cw[:, :], psO[0][:, 0:D]))
                v.sem_inc(mid_dve, 1)

                def heads(ap):
                    return ap.rearrange("p (h d) -> p h d", h=HEADS)

                def query_norm(t, u, link):
                    v.wait_ge(q_ev, t + 1)
                    q, top, tot = qsl[:, u, :], small[:, 8:12], small[:, 12:16]
                    link.done(nc.vector.tensor_reduce(top, heads(q), AX.X, ALU.max))
                    nc.vector.tensor_tensor(heads(q), heads(q), top.unsqueeze(2).to_broadcast([P, HEADS, DH]),
                                            ALU.subtract).then_inc(q_sub, 1)
                    v.wait_ge(q_exp, t + 1)
                    link.done(nc.vector.tensor_reduce(tot, heads(q), AX.X, ALU.add))
                    link.done(nc.vector.reciprocal(tot, tot))
                    nc.vector.tensor_tensor(heads(ksl[:, u, :]), heads(q),
                                            tot.unsqueeze(2).to_broadcast([P, HEADS, DH]), ALU.mult).then_inc(q_n, 1)

                def out_row(t, u):
                    v.wait_ge(o_ps, t + 1)
                    nc.vector.tensor_tensor(o_all[:, bass.ds(t, 1), :].rearrange("p a f -> p (a f)"),
                                            psO[u][:, 0:D], bout[:, :], ALU.add).then_inc(o_ok, 1)

                LINKS = 3

                def step(i, j, g, link):
                    t = j if i is None else i * UN + j
                    if g < T:
                        pair(0 if i is None else i, (1, TB), j, lambda: query_norm(t, j % 2, link))
                    if g > 1:
                        out_row(t - 2, j % 2)

                start = ch.n
                for j in range(UN):
                    step(None, j, j, ch)
                with nc.vector.Fori(1, U) as i:
                    for u in range(UN):
                        step(i, u, UN, Chain(v, dv, i * (UN * LINKS) + (start + u * LINKS)))
                ch = Chain(v, dv, start + (T - 1) * LINKS)
                for j in range(T - 1, T + 2):
                    step(None, j, j, ch)

                v.wait_ge(sq_ok, T)
                ch.done(nc.vector.tensor_scalar(sc[:, :], ssq[:, :], 1e-24, None, ALU.max))
                v.sem_inc(root_in, 1)
                v.wait_ge(root_ok, 1)
                ch.done(nc.vector.reciprocal(rs[:, :], sa[:, :]))
                ch.done(nc.vector.tensor_tensor(sd[:, :], rs[:, :], rs[:, :], ALU.mult))
                ch.done(nc.vector.tensor_tensor(sd[:, :], sd[:, :], sc[:, :], ALU.mult))
                ch.done(nc.vector.tensor_scalar(sd[:, :], sd[:, :], -0.5, 1.5, ALU.mult, ALU.add))
                ch.done(nc.vector.scalar_tensor_tensor(rs[:, :], rs[:, :], float(D) ** 0.5, sd[:, :], ALU.mult,
                                                       ALU.mult))
                v.sem_inc(res_ok, 4)

                def residual(t, u):
                    row = o_all[:, bass.ds(t, 1), :].rearrange("p a f -> p (a f)")
                    nc.vector.scalar_tensor_tensor(row, row, rs[:, bass.ds(t, 1)], gout[:, :], ALU.mult,
                                                   ALU.mult).then_inc(on_ok, 1)
                    v.wait_ge(xb_ok, t + 1)
                    v.wait_ge(on_ok, t + 1)
                    nc.vector.tensor_tensor(row, row, slot[:, u, :], ALU.add).then_inc(res_ok, 1)

                with nc.vector.Fori(0, U) as i:
                    for u in range(UN):
                        pair(i, (1, TD), u, lambda: residual(i * UN + u, u))
                pair(0, (1, TD), T - 1, lambda: residual(T - 1, 0))

        over(phase)

        phase = []
        with nc.Block() as block:
            rows_in = [semaphore(phase, f"s_rows{k}") for k in range(GC)]
            idx_ok = semaphore(phase, "s_indices")
            turns = semaphore(phase, "s_turns")
            hot_ok = semaphore(phase, "s_onehots")
            prod_ok = semaphore(phase, "s_products")
            sum_ok = semaphore(phase, "s_added")
            dv = semaphore(phase, "s_dve_order")
            dcur = small[:, 16:16 + GC]

            @block.gpsimd
            def _(pool):
                flag = nc.gpsimd.value_load(flag_i[0:1, 0:1], min_val=0, max_val=1)
                with nc.gpsimd.If(flag > 0):
                    with nc.gpsimd.Fori(0, NG) as g:
                        pool.wait_ge(sum_ok, g * SW + 1)
                        nc.gpsimd.tensor_copy(idxb[:, 0, 0:GC], srci[:, bass.ds(g, 1), :].rearrange("p g c -> p (g c)"))\
                            .then_inc(idx_ok, 1)
                        pool.wait_ge(idx_ok, g + 1)
                        pool.sem_inc(turns, 1)
                        for c in range(GC):
                            nc.gpsimd.indirect_dma_start(
                                out=grows[:, c, :], out_offset=None, in_=table,
                                in_offset=bass.IndirectOffsetOnAxis(ap=idxb[:, 0, c:c + 1], axis=0),
                            ).then_inc(rows_in[c], 16)
                        for c in range(GC):
                            pool.wait_ge(rows_in[c], g * 16 + 16)

            @block.tensor
            def _(pe):
                flag = nc.tensor.value_load(flag_i[0:1, 0:1], min_val=0, max_val=1)
                with nc.tensor.If(flag > 0):
                    with nc.tensor.Fori(0, NG) as g:
                        for c in range(GC):
                            pe.wait_ge(rows_in[c], g * 16 + 16)
                        for c in range(GC):
                            pe.wait_ge(rows_in[c], g * 16 + 16)
                        pe.sem_inc(turns, 1)
                        with nc.tensor.Fori(0, SW) as w:
                            pe.wait_ge(hot_ok, g * SW + w + 1)
                            for h in range(KC):
                                for c in range(GC):
                                    last = nc.tensor.matmul(window(2)[:, h, :], grows[:, c, h * P:(h + 1) * P],
                                                            S_t[:, 0, c, :], start=c == 0, stop=c == GC - 1)
                            last.then_inc(prod_ok, 1)

            @block.vector
            def _(v):
                v.sem_inc(sum_ok, 1)
                flag = nc.vector.value_load(flag_i[0:1, 0:1], min_val=0, max_val=1)
                with nc.vector.If(flag > 0):
                    with nc.vector.Fori(0, NG) as g:
                        nc.vector.tensor_copy(dcur, dslow[:, bass.ds(g, 1), :].rearrange("p g c -> p (g c)"))\
                            .then_inc(dv, 1)
                        v.wait_ge(dv, g * (2 * SW + 1) + 1)
                        v.sem_inc(turns, 1)
                        with nc.vector.Fori(0, SW) as w:
                            nc.vector.tensor_tensor(S_t[:, 0, :, :], dcur.unsqueeze(2).to_broadcast([P, GC, WIN]),
                                                    iwin[:, 0:WIN].unsqueeze(1).to_broadcast([P, GC, WIN]),
                                                    ALU.is_equal).then_inc(hot_ok, 1)
                            v.wait_ge(hot_ok, g * SW + w + 1)
                            nc.vector.tensor_scalar(dcur, dcur, float(-WIN), None, ALU.add).then_inc(dv, 1)
                            v.wait_ge(prod_ok, g * SW + w + 1)
                            win = acc[:, :, bass.ds(w * WIN, WIN)]
                            nc.vector.tensor_tensor(win, win, window(2), ALU.add).then_inc(dv, 1)
                            v.wait_ge(dv, g * (2 * SW + 1) + w * 2 + 3)
                            v.sem_inc(sum_ok, 1)

        over(phase)

        aw, bw, a1 = gw[:, 0, :], gw[:, 1, :], small[:, 20:21]
        tot2 = small[:, 24:26]

        phase = []
        with nc.Block() as block:
            at_ok = semaphore(phase, "c_tile_copied")
            pr_ok = semaphore(phase, "c_products")
            y_ok = semaphore(phase, "c_rows_ready")
            root_in = semaphore(phase, "c_root_in")
            root_ok = semaphore(phase, "c_root_done")
            dv = semaphore(phase, "c_dve_order")
            part = semaphore(phase, "c_partial_sums")
            whole = semaphore(phase, "c_total_sums")

            @block.scalar
            def _(act):
                def tile(t, u):
                    act.wait_ge(pr_ok, t + 1)
                    act.activation(slot[:, u, :].rearrange("p (k n) -> p k n", k=KC), acc[:, :, bass.ds(t * P, P)],
                                   ACT.Copy).then_inc(at_ok, 1)

                with nc.scalar.Fori(0, U) as i:
                    for u in range(UN):
                        tile(i * UN + u, u)
                tile(T - 1, 0)
                act.wait_ge(root_in, 1)
                act.activation(small[:, 30:31], small[:, 31:32], ACT.Sqrt).then_inc(root_ok, 1)

            @block.tensor
            def _(pe):
                pe.sem_inc(pr_ok, 4)

                def tile(t, u):
                    pe.wait_ge(at_ok, t + 1)
                    pe.wait_ge(y_ok, t + 1)
                    for k in range(KC):
                        last = nc.tensor.matmul(ps[u][:, 0:D], slot[:, u, k * P:(k + 1) * P], gw[:, k, :],
                                                start=k == 0, stop=k == KC - 1)
                    last.then_inc(pr_ok, 1)

                with nc.tensor.Fori(0, U) as i:
                    for u in range(UN):
                        tile(i * UN + u, u)
                tile(T - 1, 0)
                for n in range(2):
                    pe.wait_ge(part, n + 1)
                    nc.tensor.matmul(ps[4][:, n:n + 1], ones[:, :], small[:, 24 + n:25 + n], start=True,
                                     stop=True).then_inc(whole, 1)

            @block.vector
            def _(v):
                v.sem_inc(y_ok, 4)
                ch = Chain(v, dv)

                def rows(t, u):
                    v.wait_ge(pr_ok, t + 5)
                    nc.vector.scalar_tensor_tensor(y_all[:, bass.ds(t, 1), :].rearrange("p a f -> p (a f)"),
                                                   ps[u][:, 0:D], dinv[:, bass.ds(t, 1)], cbias[:, :],
                                                   ALU.mult, ALU.add).then_inc(y_ok, 1)

                def row_stats(t):
                    v.wait_ge(y_ok, t + 5)
                    return nc.vector.bn_stats(stats[:, bass.ds(t, 1), :].rearrange("p a f -> p (a f)"),
                                              y_all[:, bass.ds(t, 1), :].rearrange("p a f -> p (a f)"))

                rows(0, 0)
                with nc.vector.Fori(0, U) as i:
                    for u in range(UN):
                        rows(i * UN + (u + 1), (u + 1) % UN)
                        row_stats(i * UN + u)
                ch.done(row_stats(T - 1))
                most, full = float((T - 1) * D), 1.0 / (N * D)
                pm, tm = small[:, 32:34], small[:, 34:36]
                ch.done(nc.vector.bn_aggr(pm, stats[:, 0:T - 1, :].rearrange("p t s -> p (t s)")))
                ch.done(nc.vector.bn_aggr(tm, stats[:, T - 1, :]))
                ch.done(nc.vector.tensor_scalar(tm[:, 0:1], tm[:, 0:1], valid[:, :], float(D), ALU.mult, ALU.mult))
                ch.done(nc.vector.scalar_tensor_tensor(tot2[:, 0:1], pm[:, 0:1], most, tm[:, 0:1], ALU.mult, ALU.add))
                v.sem_inc(part, 1)
                ch.done(nc.vector.tensor_scalar(tm[:, 0:1], tm[:, 0:1], 1.0 / D, None, ALU.mult))
                v.wait_ge(whole, 1)
                mu = small[:, 36:37]
                ch.done(nc.vector.tensor_scalar(mu, ps[4][:, 0:1], full, None, ALU.mult))
                d1, d2 = small[:, 37:38], small[:, 38:39]
                ch.done(nc.vector.tensor_tensor(d1, pm[:, 0:1], mu, ALU.subtract))
                ch.done(nc.vector.tensor_tensor(d1, d1, d1, ALU.mult))
                ch.done(nc.vector.tensor_tensor(d1, d1, pm[:, 1:2], ALU.add))
                ch.done(nc.vector.tensor_tensor(d2, tm[:, 0:1], mu, ALU.subtract))
                ch.done(nc.vector.tensor_tensor(d2, d2, d2, ALU.mult))
                ch.done(nc.vector.tensor_tensor(d2, d2, tm[:, 1:2], ALU.add))
                ch.done(nc.vector.tensor_scalar(d2, d2, valid[:, :], float(D), ALU.mult, ALU.mult))
                ch.done(nc.vector.scalar_tensor_tensor(tot2[:, 1:2], d1, most, d2, ALU.mult, ALU.add))
                v.sem_inc(part, 1)
                v.wait_ge(whole, 2)
                val, root = small[:, 31:32], small[:, 30:31]
                ch.done(nc.vector.tensor_scalar(val, ps[4][:, 1:2], full, 1e-30, ALU.mult, ALU.max))
                v.sem_inc(root_in, 1)
                v.wait_ge(root_ok, 1)
                ch.done(nc.vector.reciprocal(d1, root))
                ch.done(nc.vector.tensor_tensor(d1, d1, val, ALU.mult))
                ch.done(nc.vector.tensor_tensor(d1, d1, root, ALU.add))
                ch.done(nc.vector.tensor_scalar(d1, d1, 0.5, EPS, ALU.mult, ALU.add))
                ch.done(nc.vector.reciprocal(d2, d1))
                ch.done(nc.vector.tensor_scalar(aw, lnw[:, :], d2, None, ALU.mult))
                ch.done(nc.vector.tensor_scalar(bw, aw, mu, None, ALU.mult))
                ch.done(nc.vector.tensor_tensor(bw, lnb[:, :], bw, ALU.subtract))
                ch.done(nc.vector.tensor_scalar(a1, pre[:, :], -1.0, 1.0, ALU.mult, ALU.add))

        over(phase)

        w2_sb = R3[:, 0:NX * HC * D].rearrange("p (e h f) -> p e h f", e=NX, h=HC)
        room = NX * HC * D

        def lanes(k):
            return R3[:, room + k * T * NX:room + (k + 1) * T * NX].rearrange("p (t e) -> p t e", e=NX)

        L, M1, M2, MM, LA, LB, LC, LD = (lanes(k) for k in range(8))
        rt = R3[:, room + 8 * T * NX:]
        top, sec, w1c, w2c = rt[:, 0:T], rt[:, T:2 * T], x1s, x1b
        r8, eb = rt[:, 2 * T:2 * T + NX], rt[:, 2 * T + NX:2 * T + 2 * NX]
        tl, cumt = rt[:, 2 * T + 2 * NX:2 * T + 3 * NX], rt[:, 2 * T + 3 * NX:2 * T + 4 * NX]
        cnt = rt[:, 2 * T + 5 * NX:2 * T + 6 * NX]
        mask, eidf = (rt[:, 160 + 128 * k:160 + 128 * k + NSTEP] for k in range(2))
        flat = S_t[:, :, :, :].rearrange("p s c w -> p (s c w)")
        ints = flat.bitcast(i32)
        gat, sct, eid_i = ints[:, 0:NTILE], ints[:, NTILE:2 * NTILE], ints[0:1, 2 * NTILE:2 * NTILE + NSTEP]
        tag_i, dump_i = ints[:, 320:320 + 2 * T], ints[:, 320 + 2 * T:320 + 2 * T + NTILE]
        tag = flat[:, 530:530 + 2 * T]
        dump = flat[:, 640:640 + NTILE]
        posf, hif, lof = (rt[:, 500 + 100 * k:500 + 100 * k + 2 * T] for k in range(3))
        pos_i, part_i = (rt[:, 800 + 100 * k:800 + 100 * k + 2 * T].bitcast(i32) for k in range(2))
        pad = rt[:, 1000:1000 + NTILE]
        held = rt[:, 1110:1110 + NTILE]
        held_i = rt[:, 1220:1220 + NTILE].bitcast(i32)
        lo1 = [R2[:, n * IB * P:(n + 1) * IB * P].rearrange("p (c j) -> p c j", c=IB) for n in range(NB)]
        hi1 = [R2[:, NB * IB * P + n * IB * NTILE:NB * IB * P + (n + 1) * IB * NTILE]
               .rearrange("p (c j) -> p c j", c=IB) for n in range(NB)]
        uT = [grows[:, 4 + k, :] for k in range(2)]
        zero_c = grows[:, 6, 0:P]

        phase = []
        with nc.Block() as block:
            w2_in = semaphore(phase, "r_w2_in")
            y1 = semaphore(phase, "r_scaled")
            y2 = semaphore(phase, "r_shifted")
            ng_ok = semaphore(phase, "r_negative_part")
            xa_ok = semaphore(phase, "r_residual_added")
            x_ok = semaphore(phase, "r_x1_ready")
            st_ok = semaphore(phase, "r_stats")
            root_in = semaphore(phase, "r_root_in")
            root_ok = semaphore(phase, "r_root_done")
            dv = semaphore(phase, "r_dve_order")
            aff = semaphore(phase, "r_affine")
            n_ok = semaphore(phase, "r_n_ready")
            keep = [semaphore(phase, f"r_n_kept{k}") for k in range(4)]
            f_ps = semaphore(phase, "r_nT_psum")
            f_ok = semaphore(phase, "r_nT_ready")
            l_ps = semaphore(phase, "r_logits_psum")
            l_ok = semaphore(phase, "r_logits")
            ex_in = semaphore(phase, "r_exp_in")
            ex_ok = semaphore(phase, "r_exp_done")
            hot = semaphore(phase, "r_choices")
            rank = semaphore(phase, "r_ranks_psum")
            pl = semaphore(phase, "r_pool_order")
            tags = semaphore(phase, "r_tags")
            pl_hot = semaphore(phase, "r_place_onehots")
            pl_tag = [semaphore(phase, f"r_place_onehots_tagged{k}") for k in range(NB)]
            pl_free = semaphore(phase, "r_place_onehots_free")
            inv_ok = semaphore(phase, "r_inverse_psum")

            @block.sync
            def _(sp):
                sp.dma_start(R3[:, 0:room], a_w2).then_inc(w2_in, 16)

                def keep_tile(t, u):
                    sp.wait_ge(n_ok, t + 1)
                    sp.dma_start(table[bass.ds(t * P, P), :], slot[:, u, :]).then_inc(keep[u], 16)

                with nc.sync.Fori(0, U) as i:
                    for u in range(UN):
                        keep_tile(i * UN + u, u)
                sp.wait_ge(n_ok, T)
                sp.dma_start(table[(T - 1) * P:N, :], slot[0:TAIL, 0, :]).then_inc(keep[0], 16)
                for u in range(UN):
                    sp.wait_ge(keep[u], 16 * (U + (1 if u == 0 else 0)))
                sp.wait_ge(w2_in, 16)

            @block.scalar
            def _(act):
                def negative(t, u):
                    act.wait_ge(y2, t + 1)
                    act.activation(slotb[:, u % 2, :], slot[:, 2 + u % 2, :], ACT.Relu, scale=-1.0).then_inc(ng_ok, 1)

                with nc.scalar.Fori(0, U) as i:
                    for u in range(UN):
                        negative(i * UN + u, u)
                negative(T - 1, 0)
                for n in range(2):
                    act.wait_ge(root_in, n + 1)
                    act.activation(sa[:, :], sc[:, :], ACT.Sqrt).then_inc(root_ok, 1)
                act.wait_ge(aff, 1)

                def norm(t, u, turn):
                    if not (isinstance(turn, int) and turn == 0):
                        act.wait_ge(keep[u], turn * 16)
                        act.wait_ge(f_ps, t - 3)
                    act.activation(slot[:, u, :], o_all[:, bass.ds(t, 1), :].rearrange("p a f -> p (a f)"),
                                   ACT.Identity, scale=zs_s[:, bass.ds(t, 1)],
                                   bias=zs_b[:, bass.ds(t, 1)]).then_inc(n_ok, 1)

                for u in range(UN):
                    norm(u, u, 0)
                with nc.scalar.Fori(1, U) as i:
                    for u in range(UN):
                        norm(i * UN + u, u, i)
                norm(T - 1, 0, U)
                act.wait_ge(ex_in, 1)
                act.activation(w2c[:, :], sec, ACT.Exp).then_inc(ex_ok, 1)
                act.wait_ge(tags, 2)
                with nc.scalar.Fori(0, 2) as i:
                    for n in range(1, NB, 2):
                        act.wait_ge(pl_hot, i * NB + (n + 1))
                        for c in range(IB):
                            last = act.activation(hi1[n][:, c, :], hi1[n][:, c, :], ACT.Copy,
                                                  scale=tag[:, bass.ds(i * (NB * IB) + (n * IB + c), 1)])
                        last.then_inc(pl_tag[n], 1)

            @block.gpsimd
            def _(pool):
                def residual(t, u):
                    pool.wait_ge(y2, t + 1)
                    row = o_all[:, bass.ds(t, 1), :].rearrange("p a f -> p (a f)")
                    nc.gpsimd.tensor_tensor(row, row, slot[:, 2 + u % 2, :], ALU.add).then_inc(xa_ok, 1)

                with nc.gpsimd.Fori(0, U) as i:
                    for u in range(UN):
                        residual(i * UN + u, u)
                residual(T - 1, 0)
                nc.gpsimd.iota(tag_i, pattern=[[2 * P, T], [1, 2]], base=1, channel_multiplier=2).then_inc(pl, 1)
                nc.gpsimd.iota(dump_i, pattern=[[P, NTILE]], base=2 * N + 1, channel_multiplier=1).then_inc(pl, 1)
                pool.wait_ge(pl, 2)
                nc.gpsimd.tensor_copy(tag, tag_i).then_inc(tags, 1)
                nc.gpsimd.tensor_copy(dump, dump_i).then_inc(tags, 1)
                pool.wait_ge(tags, 2)
                with nc.gpsimd.Fori(0, 2) as i:
                    for n in range(0, NB, 2):
                        pool.wait_ge(pl_hot, i * NB + (n + 1))
                        nc.gpsimd.tensor_tensor(hi1[n], hi1[n], tag[:, bass.ds((i * NB + n) * IB, IB)].unsqueeze(2)
                                                .to_broadcast([P, IB, NTILE]), ALU.mult).then_inc(pl_tag[n], 1)

            @block.tensor
            def _(pe):
                def flip(t, u):
                    pe.wait_ge(n_ok, t + 1)
                    pe.wait_ge(f_ok, t + 1)
                    for k in range(KC):
                        last = nc.tensor.transpose(ps[u % 2][:, k * P:(k + 1) * P], slot[:, u, k * P:(k + 1) * P],
                                                   ident[:, :])
                    last.then_inc(f_ps, 1)

                def logits(t, u):
                    pe.wait_ge(f_ok, t + 3)
                    pe.wait_ge(l_ok, t + 1)
                    for k in range(KC):
                        last = nc.tensor.matmul(ps[2 + u % 2][:, 0:NX], uT[u % 2][:, k * P:(k + 1) * P], wr[:, k, :],
                                                start=k == 0, stop=k == KC - 1)
                    last.then_inc(l_ps, 1)

                flip(0, 0)
                with nc.tensor.Fori(0, U) as i:
                    for u in range(UN):
                        flip(i * UN + (u + 1), (u + 1) % UN)
                        logits(i * UN + u, u)
                logits(T - 1, 0)
                pe.wait_ge(hot, 1)
                nc.tensor.matmul(ps[4][:, 0:T * NX], tri[:, :], MM.rearrange("p t e -> p (t e)"), start=True, stop=True)
                nc.tensor.matmul(ps[5][:, 0:T * NX], ones[:, :], MM.rearrange("p t e -> p (t e)"), start=True,
                                 stop=True).then_inc(rank, 1)
                pe.sem_inc(pl_free, NB)
                nc.tensor.matmul(ps[6][:, 0:NTILE], zero_c, zero_c[:, 0:NTILE], start=True, stop=False)
                with nc.tensor.Fori(0, 2) as i:
                    for n in range(NB):
                        pe.wait_ge(pl_tag[n], i + 1)
                        for c in range(IB):
                            last = nc.tensor.matmul(ps[6][:, 0:NTILE], lo1[n][:, c, :], hi1[n][:, c, :],
                                                    start=False, stop=False)
                        last.then_inc(pl_free, 1)
                nc.tensor.matmul(ps[6][:, 0:NTILE], zero_c, zero_c[:, 0:NTILE], start=False,
                                 stop=True).then_inc(inv_ok, 1)

            @block.vector
            def _(v):
                nc.vector.memset(zero_c, 0.0)
                v.sem_inc(x_ok, 2)
                v.sem_inc(f_ok, 2)
                v.sem_inc(l_ok, 2)

                def scale(t):
                    row = y_all[:, bass.ds(t, 1), :].rearrange("p a f -> p (a f)")
                    nc.vector.tensor_tensor(row, row, aw, ALU.mult).then_inc(y1, 1)

                def shift(t, u):
                    v.wait_ge(y1, t + 1)
                    if not (isinstance(t, int) and t < 2):
                        v.wait_ge(xa_ok, t - 1)
                    nc.vector.tensor_tensor(slot[:, 2 + u, :], y_all[:, bass.ds(t, 1), :].rearrange("p a f -> p (a f)"),
                                            bw, ALU.add).then_inc(y2, 1)

                def finish(t, u):
                    v.wait_ge(ng_ok, t + 1)
                    v.wait_ge(xa_ok, t + 1)
                    row = o_all[:, bass.ds(t, 1), :].rearrange("p a f -> p (a f)")
                    nc.vector.scalar_tensor_tensor(row, slotb[:, u, :], a1, row, ALU.mult, ALU.add).then_inc(x_ok, 1)

                def row_stats(t):
                    v.wait_ge(x_ok, t + 3)
                    nc.vector.bn_stats(stats[:, bass.ds(t, 1), :].rearrange("p a f -> p (a f)"),
                                       o_all[:, bass.ds(t, 1), :].rearrange("p a f -> p (a f)")).then_inc(st_ok, 1)

                def step(t, j):
                    if j < T - 3:
                        scale(t + 3)
                    if 0 <= j:
                        row_stats(t)
                    if -2 <= j < T - 2:
                        shift(t + 2, j % 2)
                    if -1 <= j < T - 1:
                        finish(t + 1, (j + 1) % 2)

                for t in range(-3, UN):
                    step(t, t)
                with nc.vector.Fori(1, U - 1) as i:
                    for u in range(UN):
                        step(i * UN + u, UN + u)
                for t in range(T - 1 - UN, T):
                    step(t, t)
                v.wait_ge(st_ok, T)
                ch = Chain(v, dv)
                for t in range(T):
                    last = nc.vector.bn_aggr(mv[:, t, :], stats[:, t, :])
                ch.done(last)
                mean, var = mv[:, :, 0], mv[:, :, 1]

                def rsqrt(out, val, count):
                    v.sem_inc(root_in, 1)
                    v.wait_ge(root_ok, count)
                    ch.done(nc.vector.reciprocal(out, sa[:, :]))
                    ch.done(nc.vector.tensor_tensor(sd[:, :], out, out, ALU.mult))
                    ch.done(nc.vector.tensor_tensor(sd[:, :], sd[:, :], val, ALU.mult))
                    ch.done(nc.vector.tensor_scalar(sd[:, :], sd[:, :], -0.5, 1.5, ALU.mult, ALU.add))
                    ch.done(nc.vector.tensor_tensor(out, out, sd[:, :], ALU.mult))

                ch.done(nc.vector.tensor_scalar(sc[:, :], var, EPS, None, ALU.add))
                rsqrt(zs_s[:, :], sc[:, :], 1)
                ch.done(nc.vector.tensor_tensor(sc[:, :], zs_s[:, :], zs_s[:, :], ALU.mult))
                ch.done(nc.vector.tensor_tensor(sc[:, :], sc[:, :], var, ALU.mult))
                ch.done(nc.vector.tensor_scalar(sc[:, :], sc[:, :], EPS, None, ALU.add))
                rsqrt(rstd[:, :], sc[:, :], 2)
                ch.done(nc.vector.tensor_tensor(zs_s[:, :], zs_s[:, :], rstd[:, :], ALU.mult))
                ch.done(nc.vector.scalar_tensor_tensor(zs_b[:, :], mean, -1.0, zs_s[:, :], ALU.mult, ALU.mult))
                v.sem_inc(aff, 1)

                def widen(t, u):
                    v.wait_ge(f_ps, t + 1)
                    for k in range(KC):
                        last = nc.vector.tensor_scalar(uT[u % 2][:, k * P:(k + 1) * P], ps[u % 2][:, k * P:(k + 1) * P],
                                                       gamma[:, k:k + 1], beta[:, k:k + 1], ALU.mult, ALU.add)
                    last.then_inc(f_ok, 1)

                def collect(t, u):
                    v.wait_ge(l_ps, t + 1)
                    nc.vector.tensor_tensor(L[:, bass.ds(t, 1), :].rearrange("p a f -> p (a f)"),
                                            ps[2 + u % 2][:, 0:NX], brr[:, :], ALU.add).then_inc(l_ok, 1)

                widen(0, 0)
                with nc.vector.Fori(0, U) as i:
                    for u in range(UN):
                        widen(i * UN + (u + 1), (u + 1) % 2)
                        collect(i * UN + u, u % 2)
                collect(T - 1, 0)
                v.wait_ge(l_ok, T + 2)

                shape = [P, T, NX]

                def over_e(ap):
                    return ap.unsqueeze(2).to_broadcast(shape)

                ch.done(nc.vector.tensor_scalar(r8, iwin[:, 0:NX], -1.0, float(NX), ALU.mult, ALU.add))

                def choose(out, logit, peak, tmp):
                    ch.done(nc.vector.tensor_reduce(peak, logit, AX.X, ALU.max))
                    ch.done(nc.vector.tensor_tensor(tmp, logit, over_e(peak), ALU.is_equal))
                    ch.done(nc.vector.tensor_tensor(tmp, tmp, r8.unsqueeze(1).to_broadcast(shape), ALU.mult))
                    ch.done(nc.vector.tensor_reduce(mask[:, 0:T], tmp, AX.X, ALU.max))
                    ch.done(nc.vector.tensor_tensor(out, tmp, over_e(mask[:, 0:T]), ALU.is_equal))

                choose(M1, L, top, LA)
                ch.done(nc.vector.scalar_tensor_tensor(LB, M1, -1e30, L, ALU.mult, ALU.add))
                choose(M2, LB, sec, LA)
                ch.done(nc.vector.tensor_tensor(MM, M1, M2, ALU.add))
                ch.done(nc.vector.tensor_scalar(MM[:, T - 1, :], MM[:, T - 1, :], valid[:, :], None, ALU.mult))
                v.sem_inc(hot, 1)
                ch.done(nc.vector.tensor_tensor(sec, sec, top, ALU.subtract))
                v.sem_inc(ex_in, 1)
                v.wait_ge(ex_ok, 1)
                ch.done(nc.vector.tensor_scalar(w1c[:, :], w2c[:, :], 1.0, None, ALU.add))
                ch.done(nc.vector.reciprocal(w1c[:, :], w1c[:, :]))
                ch.done(nc.vector.tensor_tensor(w2c[:, :], w2c[:, :], w1c[:, :], ALU.mult))
                v.wait_ge(rank, 1)
                total = ps[5][:, 0:T * NX].rearrange("p (t e) -> p t e", e=NX)
                within = ps[4][:, 0:T * NX].rearrange("p (t e) -> p t e", e=NX)
                ch.done(nc.vector.tensor_copy(LA, total))
                a, b, s = LA, LB, 1
                while s < T:
                    nc.vector.tensor_copy(b[:, 0:s, :], a[:, 0:s, :])
                    ch.done(nc.vector.tensor_tensor(b[:, s:T, :], a[:, s:T, :], a[:, 0:T - s, :], ALU.add))
                    a, b, s = b, a, 2 * s
                ch.done(nc.vector.tensor_copy(cnt, a[:, T - 1, :]))
                ch.done(nc.vector.tensor_scalar(mask[:, 0:T], iwin[:, 0:T], float(P), None, ALU.mult))
                ev = LD.rearrange("p t e -> p (t e)").rearrange("p (e t) -> p e t", e=NX)
                ch.done(nc.vector.tensor_tensor(ev, cnt.unsqueeze(2).to_broadcast([P, NX, T]),
                                                mask[:, 0:T].unsqueeze(1).to_broadcast([P, NX, T]), ALU.is_gt))
                ch.done(nc.vector.tensor_reduce(tl, ev, AX.X, ALU.add))
                ch.done(nc.vector.tensor_copy(cumt, tl))
                for e in range(1, NX):
                    ch.done(nc.vector.tensor_tensor(cumt[:, e:e + 1], cumt[:, e:e + 1], cumt[:, e - 1:e], ALU.add))
                ch.done(nc.vector.tensor_tensor(eb, cumt, tl, ALU.subtract))
                ch.done(nc.vector.tensor_scalar(eb, eb, float(P), None, ALU.mult))
                ch.done(nc.vector.tensor_tensor(LC, a, total, ALU.subtract))
                ch.done(nc.vector.tensor_tensor(LC, LC, within, ALU.add))
                ch.done(nc.vector.tensor_tensor(LC, LC, eb.unsqueeze(1).to_broadcast(shape), ALU.add))
                pk = posf.rearrange("p (t k) -> p t k", k=2)
                for k, m in ((0, M1), (1, M2)):
                    ch.done(nc.vector.tensor_tensor(LD, LC, m, ALU.mult))
                    ch.done(nc.vector.tensor_reduce(pk[:, :, k], LD, AX.X, ALU.add))
                ch.done(nc.vector.tensor_copy(pos_i, posf))
                ch.done(nc.vector.tensor_scalar(part_i, pos_i, 7, None, ALU.arith_shift_right))
                ch.done(nc.vector.tensor_copy(hif, part_i))
                ch.done(nc.vector.tensor_scalar(part_i, pos_i, P - 1, None, ALU.bitwise_and))
                ch.done(nc.vector.tensor_copy(lof, part_i))
                late = hif[:, 2 * T - 2:2 * T]
                ch.done(nc.vector.tensor_scalar(late, late, 1.0, valid[:, :], ALU.add, ALU.mult))
                ch.done(nc.vector.tensor_scalar(late, late, -1.0, None, ALU.add))
                with nc.vector.Fori(0, 2) as i:
                    for n in range(NB):
                        m = i * NB + n
                        v.wait_ge(pl_free, m + 1)
                        nc.vector.tensor_tensor(hi1[n], hif[:, bass.ds(m * IB, IB)].unsqueeze(2)
                                                .to_broadcast([P, IB, NTILE]), iwin[:, 0:NTILE].unsqueeze(1)
                                                .to_broadcast([P, IB, NTILE]), ALU.is_equal)
                        nc.vector.tensor_tensor(lo1[n], lof[:, bass.ds(m * IB, IB)].unsqueeze(2)
                                                .to_broadcast([P, IB, P]), iwin[:, :].unsqueeze(1)
                                                .to_broadcast([P, IB, P]), ALU.is_equal).then_inc(pl_hot, 1)
                steps = iwin[:, 0:NSTEP]
                ch.done(nc.vector.memset(eidf, 0.0))
                for e in range(NX - 1):
                    ch.done(nc.vector.tensor_scalar(mask, steps, cumt[:, e:e + 1], None, ALU.is_ge))
                    ch.done(nc.vector.tensor_tensor(eidf, eidf, mask, ALU.add))
                ch.done(nc.vector.tensor_copy(eid_i, eidf[0:1, :]))
                v.wait_ge(inv_ok, 1)
                ch.done(nc.vector.tensor_copy(held, ps[6][:, 0:NTILE]))
                ch.done(nc.vector.tensor_scalar(pad, held, 0.5, None, ALU.is_lt))
                ch.done(nc.vector.tensor_tensor(pad, pad, dump, ALU.mult))
                ch.done(nc.vector.scalar_tensor_tensor(pad, held, -1.0, pad, ALU.add, ALU.add))
                ch.done(nc.vector.tensor_copy(sct, pad))
                ch.done(nc.vector.tensor_scalar(held, held, -1.0, 0.0, ALU.add, ALU.max))
                ch.done(nc.vector.tensor_copy(held_i, held))
                ch.done(nc.vector.tensor_scalar(gat, held_i, 1, None, ALU.arith_shift_right))

        over(phase)

        w1r = RG[:, :].rearrange("p (s f) -> p s f", s=4)
        xr = R2[:, 0:4 * D].rearrange("p (s f) -> p s f", s=4)
        yr = R2[:, 4 * D:8 * D].rearrange("p (s f) -> p s f", s=4)
        ur = R2[:, 8 * D:10 * D].rearrange("p (s k n) -> p s k n", s=2, k=KC)
        hr = R2[:, 10 * D:10 * D + 2 * HID].rearrange("p (s h n) -> p s h n", s=2, h=HC)
        b2s = R2[:, 16 * D:16 * D + NX * D].rearrange("p (e f) -> p e f", e=NX)

        phase = []
        with nc.Block() as block:
            b2_in = semaphore(phase, "e_b2_in")
            x_in = [semaphore(phase, f"e_x{k}") for k in range(4)]
            w_in = [semaphore(phase, f"e_w{k}") for k in range(4)]
            xt_ps = semaphore(phase, "e_xT_psum")
            u_ok = semaphore(phase, "e_xT_ready")
            h_ps = semaphore(phase, "e_h_psum")
            h_ok = semaphore(phase, "e_gelu")
            y_ps = semaphore(phase, "e_y_psum")
            y_ok = semaphore(phase, "e_y_ready")
            y_out = [semaphore(phase, f"e_y_stored{k}") for k in range(4)]
            idx_ok = semaphore(phase, "e_indices")
            turns = semaphore(phase, "e_turns")

            psX, psH, psY = [ps[0], ps[1]], [ps[2], ps[3]], [ps[4], ps[5]]
            LOOPS = (NTILE - 1) // 4

            @block.sync
            def _(sp):
                sp.dma_start(R2[:, 16 * D:16 * D + NX * D], a_b2.unsqueeze(0).to_broadcast([P, NX * D])).then_inc(b2_in, 16)

                def fetch(t, s):
                    e = nc.sync.value_load(eid_i[0:1, bass.ds(t, 1)], min_val=0, max_val=NX - 1)
                    sp.wait_ge(h_ok, t + 1)
                    sp.dma_start(w1r[:, s, :], a_w1[bass.ds(e, 1), :, :].rearrange("a p f -> (a p) f")).then_inc(w_in[s], 16)

                fetch(0, 0)
                fetch(1, 1)
                with nc.sync.Fori(0, LOOPS) as i:
                    for u in range(4):
                        fetch(i * 4 + (u + 2), (u + 2) % 4)
                sp.wait_ge(b2_in, 16)
                for s in range(4):
                    sp.wait_ge(w_in[s], 16 * (LOOPS + (1 if s < 2 else 0)))

            @block.tensor
            def _(pe):
                pe.sem_inc(u_ok, 2)
                pe.sem_inc(y_ps, 2)

                def flip(t, s, turn):
                    pe.wait_ge(x_in[s], turn * 16 + 16)
                    pe.wait_ge(u_ok, t + 1)
                    for k in range(KC):
                        last = nc.tensor.transpose(psX[s % 2][:, k * P:(k + 1) * P], xr[:, s, k * P:(k + 1) * P],
                                                   ident[:, :])
                    last.then_inc(xt_ps, 1)

                def hidden(t, s, turn):
                    pe.wait_ge(w_in[s], turn * 16 + 16)
                    pe.wait_ge(u_ok, t + 3)
                    pe.wait_ge(h_ok, t + 3)
                    for h in range(HC):
                        for k in range(KC):
                            last = nc.tensor.matmul(psH[s % 2][:, h * P:(h + 1) * P],
                                                    w1r[:, s, k * HID + h * P:k * HID + (h + 1) * P],
                                                    ur[:, s % 2, k, :], start=k == 0, stop=k == KC - 1)
                    last.then_inc(h_ps, 1)

                def rows(t, s):
                    e = nc.tensor.value_load(eid_i[0:1, bass.ds(t, 1)], min_val=0, max_val=NX - 1)
                    pe.wait_ge(h_ok, t + 5)
                    pe.wait_ge(y_ok, t + 1)
                    for h in range(HC):
                        last = nc.tensor.matmul(psY[s % 2][:, 0:D], hr[:, s % 2, h, :],
                                                w2_sb[:, bass.ds(e, 1), h, :].rearrange("p a f -> p (a f)"),
                                                start=h == 0, stop=h == HC - 1)
                    last.then_inc(y_ps, 1)

                flip(0, 0, 0)
                flip(1, 1, 0)
                hidden(0, 0, 0)
                with nc.tensor.Fori(0, LOOPS) as i:
                    for u in range(4):
                        flip(i * 4 + (u + 2), (u + 2) % 4, i + (u + 2) // 4)
                        hidden(i * 4 + (u + 1), (u + 1) % 4, i + (u + 1) // 4)
                        rows(i * 4 + u, u)
                rows(NTILE - 1, 0)

            @block.scalar
            def _(act):
                act.sem_inc(h_ok, 4)

                def gelu(t, s):
                    act.wait_ge(h_ps, t + 1)
                    act.wait_ge(y_ps, t + 1)
                    for h in range(HC):
                        last = act.activation(hr[:, s % 2, h, :], psH[s % 2][:, h * P:(h + 1) * P], ACT.Gelu,
                                              bias=w1r[:, s, KC * HID + h:KC * HID + h + 1])
                    last.then_inc(h_ok, 1)

                gelu(0, 0)
                with nc.scalar.Fori(0, LOOPS) as i:
                    for u in range(4):
                        gelu(i * 4 + (u + 1), (u + 1) % 4)

            @block.vector
            def _(v):
                v.sem_inc(y_ok, 2)

                def widen(t, s):
                    v.wait_ge(xt_ps, t + 1)
                    for k in range(KC):
                        last = nc.vector.tensor_scalar(ur[:, s % 2, k, :], psX[s % 2][:, k * P:(k + 1) * P],
                                                       gamma[:, k:k + 1], beta[:, k:k + 1], ALU.mult, ALU.add)
                    last.then_inc(u_ok, 1)

                def bias(t, s, turn):
                    e = nc.vector.value_load(eid_i[0:1, bass.ds(t, 1)], min_val=0, max_val=NX - 1)
                    v.wait_ge(y_ps, t + 3)
                    if not (isinstance(turn, int) and turn == 0):
                        v.wait_ge(y_out[s], turn * 16)
                    nc.vector.tensor_tensor(yr[:, s, :], psY[s % 2][:, 0:D],
                                            b2s[:, bass.ds(e, 1), :].rearrange("p a f -> p (a f)"),
                                            ALU.add).then_inc(y_ok, 1)

                widen(0, 0)
                widen(1, 1)
                v.wait_ge(b2_in, 16)
                for t in range(4):
                    widen(t + 2, (t + 2) % 4)
                    bias(t, t, 0)
                with nc.vector.Fori(1, LOOPS) as i:
                    for u in range(4):
                        widen(i * 4 + (u + 2), (u + 2) % 4)
                        bias(i * 4 + u, u, i)
                bias(NTILE - 1, 0, LOOPS)

            @block.gpsimd
            def _(pool):
                def gather(t, s):
                    pool.wait_ge(u_ok, t - 1)
                    nc.gpsimd.tensor_copy(idxb[:, 0, s:s + 1], gat[:, bass.ds(t, 1)]).then_inc(idx_ok, 1)
                    pool.wait_ge(idx_ok, t * 2 - 6)
                    pool.sem_inc(turns, 1)
                    rows_in(s)

                def rows_in(s):
                    nc.gpsimd.indirect_dma_start(
                        out=xr[:, s, :], out_offset=None, in_=table,
                        in_offset=bass.IndirectOffsetOnAxis(ap=idxb[:, 0, s:s + 1], axis=0)).then_inc(x_in[s], 16)

                def scatter(t, s, behind=0):
                    pool.wait_ge(y_ok, t + 3)
                    nc.gpsimd.tensor_copy(idxb[:, 1, s:s + 1], sct[:, bass.ds(t, 1)]).then_inc(idx_ok, 1)
                    pool.wait_ge(idx_ok, t * 2 + (3 - behind))
                    pool.sem_inc(turns, 1)
                    nc.gpsimd.indirect_dma_start(
                        out=results, out_offset=bass.IndirectOffsetOnAxis(ap=idxb[:, 1, s:s + 1], axis=0),
                        in_=yr[:, s, :], in_offset=None).then_inc(y_out[s], 16)

                nc.gpsimd.tensor_copy(idxb[:, 0, 0:4], gat[:, 0:4]).then_inc(idx_ok, 1)
                pool.wait_ge(idx_ok, 1)
                for s in range(4):
                    rows_in(s)
                with nc.gpsimd.Fori(0, LOOPS - 1) as i:
                    for u in range(4):
                        gather(i * 4 + (u + 4), u)
                        scatter(i * 4 + u, u)
                gather(NTILE - 1, 0)
                pool.wait_ge(u_ok, NTILE - 1)
                rows_in(1)
                for n in range(5):
                    scatter(NTILE - 5 + n, n % 4, n)
                for s in range(4):
                    pool.wait_ge(y_out[s], 16 * (LOOPS + (1 if s == 0 else 0)))

        over(phase)

        RS = 8
        pairs = RG[:, 0:RS * 2 * D].rearrange("p (s f) -> p s f", s=RS)
        assert T % RS == 1

        phase = []
        with nc.Block() as block:
            got = [semaphore(phase, f"o_rows{k}") for k in range(RS)]
            mid = semaphore(phase, "o_first_added")
            ok = semaphore(phase, "o_ready")
            stored = [semaphore(phase, f"o_stored{k}") for k in range(RS)]

            @block.sync
            def _(sp):
                def load(t, s, n=P):
                    sp.dma_start(pairs[0:n, s, :], results[bass.ds(t * (2 * P), 2 * n), :]
                                 .rearrange("(p k) f -> p (k f)", k=2)).then_inc(got[s], 16)

                for s in range(RS):
                    load(s, s)
                with nc.sync.Fori(1, T // RS) as i:
                    for s in range(RS):
                        sp.wait_ge(stored[s], i * 16)
                        load(i * RS + s, s)
                sp.wait_ge(stored[0], T // RS * 16)
                load(T - 1, 0, TAIL)

            @block.vector
            def _(v):
                def combine(t, s, turn, n=P):
                    v.wait_ge(got[s], turn * 16 + 16)
                    x1 = o_all[0:n, bass.ds(t, 1), :].rearrange("p a f -> p (a f)")
                    nc.vector.scalar_tensor_tensor(slotb[0:n, s % 2, :], pairs[0:n, s, 0:D], w1c[0:n, bass.ds(t, 1)],
                                                   x1, ALU.mult, ALU.add).then_inc(mid, 1)
                    v.wait_ge(mid, t + 1)
                    nc.vector.scalar_tensor_tensor(pairs[0:n, s, 0:D], pairs[0:n, s, D:2 * D],
                                                   w2c[0:n, bass.ds(t, 1)], slotb[0:n, s % 2, :], ALU.mult,
                                                   ALU.add).then_inc(ok, 1)

                with nc.vector.Fori(0, T // RS) as i:
                    for s in range(RS):
                        combine(i * RS + s, s, i)
                combine(T - 1, 0, T // RS, TAIL)

            @block.scalar
            def _(act):
                with nc.scalar.Fori(0, T // RS) as i:
                    for s in range(RS):
                        act.wait_ge(ok, i * RS + (s + 1))
                        act.dma_start(a_out[bass.ds((i * RS + s) * P, P), :], pairs[:, s, 0:D]).then_inc(stored[s], 16)
                act.wait_ge(ok, T)
                act.dma_start(a_out[(T - 1) * P:N, :], pairs[0:TAIL, 0, 0:D]).then_inc(stored[0], 16)
                for s in range(RS):
                    act.wait_ge(stored[s], 16 * (T // RS + (1 if s == 0 else 0)))


def kernel(x, src, dst, L0_gnn_W, L0_gnn_conv_bias, L0_gnn_ln_weight, L0_gnn_ln_bias, L0_gnn_prelu_a, L0_mix_t,
           L0_mix_w_qkv, L0_mix_mem_kv, L0_mix_w_out, L0_mix_b_out, L0_mix_g_out, L0_mix_g_pre, L0_ffn_gamma,
           L0_ffn_beta, L0_ffn_Wr, L0_ffn_br, L0_ffn_W1, L0_ffn_b1, L0_ffn_W2, L0_ffn_b2):
    import numpy as np
    import concourse.bacc as bacc
    from concourse.bass_utils import run_bass_kernel_spmd

    def halves(a):
        return np.asarray(a).reshape(KC, P).T.reshape(-1)

    memory = np.asarray(L0_mix_mem_kv).reshape(2, HEADS * DH, MEM)
    w1 = np.asarray(L0_ffn_W1).reshape(NX, KC, P, HID).transpose(0, 2, 1, 3).reshape(NX, P, KC * HID)
    b1 = np.asarray(L0_ffn_b1).reshape(NX, HC, P).transpose(0, 2, 1)
    w2 = np.asarray(L0_ffn_W2).reshape(NX, HC, P, D).transpose(2, 0, 1, 3).reshape(P, NX * HC * D)
    ins = {
        "x": x, "src": src, "dst": dst, "gw": L0_gnn_W, "cb": L0_gnn_conv_bias, "lnw": L0_gnn_ln_weight,
        "lnb": L0_gnn_ln_bias, "pre": L0_gnn_prelu_a, "wqkv": L0_mix_w_qkv, "mk": memory[0], "mv": memory[1],
        "wout": L0_mix_w_out, "bout": L0_mix_b_out, "gout": L0_mix_g_out, "gpre": halves(L0_mix_g_pre),
        "gamma": halves(L0_ffn_gamma), "beta": halves(L0_ffn_beta), "wr": L0_ffn_Wr, "br": L0_ffn_br,
        "w1": np.concatenate([w1, b1], axis=2), "w2": w2, "b2": np.asarray(L0_ffn_b2).reshape(-1),
    }
    nc = bacc.Bacc("TRN2", target_bir_lowering=False, num_devices=1)
    arrays, args = {}, []
    for name, a in ins.items():
        a = np.ascontiguousarray(a)
        arrays[f"in_{name}"] = a
        args.append(nc.dram_tensor(f"in_{name}", a.shape, mybir.dt.from_np(a.dtype), kind="ExternalInput").ap())
    out = nc.dram_tensor("out", (N, D), f32, kind="ExternalOutput").ap()
    build(nc, *args, out)
    r = run_bass_kernel_spmd(nc, [arrays], core_ids=[0])
    return r.results[0]["out"]
```
